# Optimizing a Trainium2 kernel written in Bass

```python
import numpy as np
import jax
import jax.numpy as jnp

def _softmax(x, axis=-1):
    return jax.nn.softmax(x, axis=axis)

def _gelu(x):
    return jax.nn.gelu(x, approximate=True)

def _silu(x):
    return jax.nn.silu(x)

def _sigmoid(x):
    return jax.nn.sigmoid(x)

def _layernorm(x, axis=-1, eps=1e-05):
    m = jnp.mean(x, axis=axis, keepdims=True)
    v = jnp.var(x, axis=axis, keepdims=True)
    return (x - m) / jnp.sqrt(v + eps)

def _scatter_add(tgt, idx, src, axis=0):
    return tgt.at[idx].add(src)

def _segment_sum(src, seg, n):
    return jax.ops.segment_sum(src, seg, n)
kernel_name = 'mk_cond_seq_d1_seqx_r8_de44b3'

def setup_inputs(seed: int=0):
    np.random.seed(seed)
    _w = jnp.asarray

    def _rec_inputs():
        import jax
        import jax.numpy as jnp
        _rk = jax.random.key(seed)
        x = -0.0003929 + 0.9999 * jax.random.normal(jax.random.fold_in(_rk, 1), (8, 128, 256), jnp.float32)
        _lenS = 128 - jax.random.randint(jax.random.fold_in(_rk, 7), (8,), 0, max(1, 128 // 4) + 1, jnp.int32)
        _lenS2 = 128 - jax.random.randint(jax.random.fold_in(_rk, 8), (8,), 0, max(1, 128 // 4) + 1, jnp.int32)
        pos_BxS = jnp.broadcast_to(jnp.arange(128, dtype=jnp.int32), (8, 128))
        cond_2048 = 0.00782532 + 1.00527 * jax.random.normal(jax.random.fold_in(_rk, 12), (8, 256), jnp.float32)
        return (x, pos_BxS, cond_2048)
    x, pos_BxS, cond_2048 = _rec_inputs()

    def _L0_cond_setup():
        import jax, jax.numpy as jnp
        import numpy as np
        HIDDEN, NQ, NKV, HD, INTER = (256, 8, 1, 32, 1024)
        B, S = (4, 256)
        EPS = 1e-06
        ROPE_BASE = 10000.0

        def ada_rms(x, t, w, tw):
            n = x * jax.lax.rsqrt(jnp.mean(jnp.square(x), axis=-1, keepdims=True) + EPS)
            scale = t @ tw.T
            return n * (w * (1.0 + scale))[:, None, :]

        def apply_rope(x, pos_ids):
            half = HD // 2
            inv_freq = 1.0 / ROPE_BASE ** (jnp.arange(0, HD, 2, dtype=jnp.float32) / HD)
            ang = pos_ids.astype(jnp.float32)[:, :, None] * inv_freq
            cos = jnp.concatenate([jnp.cos(ang), jnp.cos(ang)], axis=-1)[:, None]
            sin = jnp.concatenate([jnp.sin(ang), jnp.sin(ang)], axis=-1)[:, None]
            x1, x2 = (x[..., :half], x[..., half:])
            rot = jnp.concatenate([-x2, x1], axis=-1)
            return x * cos + rot * sin
        key = jax.random.key(seed)
        ks = jax.random.split(key, 12)
        f32 = jnp.float32
        inp = {'x': jax.random.normal(ks[0], (B, S, HIDDEN), f32), 'pos_ids': jnp.broadcast_to(jnp.arange(S, dtype=jnp.int32), (B, S)), 'time_emb': jax.random.normal(ks[1], (B, HIDDEN), f32), 'ln1_w': jnp.ones((HIDDEN,), f32), 'ln1_tw': jax.random.normal(ks[2], (HIDDEN, HIDDEN), f32) * 0.02, 'ln2_w': jnp.ones((HIDDEN,), f32), 'ln2_tw': jax.random.normal(ks[3], (HIDDEN, HIDDEN), f32) * 0.02, 'Wq': jax.random.normal(ks[4], (NQ * HD, HIDDEN), f32) * 0.02, 'Wk': jax.random.normal(ks[5], (NKV * HD, HIDDEN), f32) * 0.02, 'Wv': jax.random.normal(ks[6], (NKV * HD, HIDDEN), f32) * 0.02, 'Wo': jax.random.normal(ks[7], (HIDDEN, NQ * HD), f32) * 0.02, 'Wg': jax.random.normal(ks[8], (INTER, HIDDEN), f32) * 0.02, 'Wu': jax.random.normal(ks[9], (INTER, HIDDEN), f32) * 0.02, 'Wd': jax.random.normal(ks[10], (HIDDEN, INTER), f32) * 0.02}
        return inp
    _L0_cond_all = _L0_cond_setup()
    _L0_cond_in = {k: v for k, v in _L0_cond_all.items() if k in ('ln1_w', 'ln1_tw', 'ln2_w', 'ln2_tw', 'Wq', 'Wk', 'Wv', 'Wo', 'Wg', 'Wu', 'Wd')}
    del _L0_cond_all
    return {'x': x, 'pos_BxS': pos_BxS, 'cond_2048': cond_2048, 'L0_cond_ln1_w': _L0_cond_in['ln1_w'], 'L0_cond_ln1_tw': _L0_cond_in['ln1_tw'], 'L0_cond_ln2_w': _L0_cond_in['ln2_w'], 'L0_cond_ln2_tw': _L0_cond_in['ln2_tw'], 'L0_cond_Wq': _L0_cond_in['Wq'], 'L0_cond_Wk': _L0_cond_in['Wk'], 'L0_cond_Wv': _L0_cond_in['Wv'], 'L0_cond_Wo': _L0_cond_in['Wo'], 'L0_cond_Wg': _L0_cond_in['Wg'], 'L0_cond_Wu': _L0_cond_in['Wu'], 'L0_cond_Wd': _L0_cond_in['Wd']}

def reference(x, pos_BxS, cond_2048, L0_cond_ln1_w, L0_cond_ln1_tw, L0_cond_ln2_w, L0_cond_ln2_tw, L0_cond_Wq, L0_cond_Wk, L0_cond_Wv, L0_cond_Wo, L0_cond_Wg, L0_cond_Wu, L0_cond_Wd):
    import jax
    import jax.numpy as jnp

    def _L0_cond_ref(x, pos_ids, time_emb, ln1_w, ln1_tw, ln2_w, ln2_tw, Wq, Wk, Wv, Wo, Wg, Wu, Wd):
        import jax, jax.numpy as jnp
        import numpy as np
        HIDDEN, NQ, NKV, HD, INTER = (256, 8, 1, 32, 1024)
        B, S = (4, 256)
        EPS = 1e-06
        ROPE_BASE = 10000.0

        def ada_rms(x, t, w, tw):
            n = x * jax.lax.rsqrt(jnp.mean(jnp.square(x), axis=-1, keepdims=True) + EPS)
            scale = t @ tw.T
            return n * (w * (1.0 + scale))[:, None, :]

        def apply_rope(x, pos_ids):
            half = HD // 2
            inv_freq = 1.0 / ROPE_BASE ** (jnp.arange(0, HD, 2, dtype=jnp.float32) / HD)
            ang = pos_ids.astype(jnp.float32)[:, :, None] * inv_freq
            cos = jnp.concatenate([jnp.cos(ang), jnp.cos(ang)], axis=-1)[:, None]
            sin = jnp.concatenate([jnp.sin(ang), jnp.sin(ang)], axis=-1)[:, None]
            x1, x2 = (x[..., :half], x[..., half:])
            rot = jnp.concatenate([-x2, x1], axis=-1)
            return x * cos + rot * sin
        b, s, _ = x.shape
        g = NQ // NKV
        res = x
        h = ada_rms(x, time_emb, ln1_w, ln1_tw)
        q = (h @ Wq.T).reshape(b, s, NQ, HD).transpose(0, 2, 1, 3)
        k = (h @ Wk.T).reshape(b, s, NKV, HD).transpose(0, 2, 1, 3)
        v = (h @ Wv.T).reshape(b, s, NKV, HD).transpose(0, 2, 1, 3)
        q = apply_rope(q, pos_ids)
        k = apply_rope(k, pos_ids)
        qg = q.reshape(b, NKV, g, s, HD)
        scores = jnp.einsum('bkgsd,bktd->bkgst', qg, k) / jnp.sqrt(jnp.float32(HD))
        attn = jax.nn.softmax(scores, axis=-1)
        ctx = jnp.einsum('bkgst,bktd->bkgsd', attn, v)
        ctx = ctx.reshape(b, NQ, s, HD).transpose(0, 2, 1, 3).reshape(b, s, NQ * HD)
        x = res + ctx @ Wo.T
        res = x
        h = ada_rms(x, time_emb, ln2_w, ln2_tw)
        mlp = jax.nn.silu(h @ Wg.T) * (h @ Wu.T) @ Wd.T
        return res + mlp
    x = _L0_cond_ref(x, pos_BxS, cond_2048, L0_cond_ln1_w, L0_cond_ln1_tw, L0_cond_ln2_w, L0_cond_ln2_tw, L0_cond_Wq, L0_cond_Wk, L0_cond_Wv, L0_cond_Wo, L0_cond_Wg, L0_cond_Wu, L0_cond_Wd)
    return x

_drawn_inputs = setup_inputs


def setup_inputs(seed=0):
    import zlib

    import numpy as np

    out = dict(_drawn_inputs(seed))
    spreads = {'L0_cond_ln1_w': (1.0, 0.6), 'L0_cond_ln2_w': (1.0, 0.6)}
    factors = {'cond_2048': 3.129,
     'L0_cond_ln1_tw': 8.0,
     'L0_cond_ln2_tw': 8.411,
     'L0_cond_Wq': 8.0,
     'L0_cond_Wk': 8.0,
     'L0_cond_Wv': 5.585,
     'L0_cond_Wo': 5.607,
     'L0_cond_Wg': 2.953,
     'L0_cond_Wu': 2.68,
     'L0_cond_Wd': 2.681}
    for name, (base, spread) in spreads.items():
        noise = np.random.default_rng([zlib.crc32(name.encode()), seed]).standard_normal(out[name].shape)
        drawn = base * np.exp(spread * noise) if base else spread * noise
        out[name] = jnp.asarray(drawn.astype(out[name].dtype))
    for name, factor in factors.items():
        out[name] = (out[name] * factor).astype(out[name].dtype)
    return out
```

```python
from contextlib import ExitStack

import numpy as np

import concourse.bass as bass
from concourse import mybir

F32 = mybir.dt.float32
F32R = mybir.dt.float32r
I32 = mybir.dt.int32
ALU = mybir.AluOpType
ACT = mybir.ActivationFunctionType
AX = mybir.AxisListType

P = 128
B, S, D = 8, 128, 256
HEADS, HD = 8, 32
INTER = 1024
EPS = 1e-6
ROPE_BASE = 10000.0

T = B * S
KT = D // P
QKV = HEADS * HD + 2 * HD
NR = HEADS + 1
HALF = HD // 2
PAIRS = B // 2
HT = T // 2
HB = B // 2
IT = INTER // P
WIDE = 512
SCALE = float(np.float32(1.0) / np.sqrt(np.float32(HD)))

TWO_PI = 2.0 * np.pi


def _cut(x, bits):
    e = np.floor(np.log2(x)) - (bits - 1)
    return float(np.floor(x / 2.0 ** e) * 2.0 ** e)


PI_1 = _cut(TWO_PI, 9)
PI_2 = _cut(TWO_PI - PI_1, 9)
PI_3 = _cut(TWO_PI - PI_1 - PI_2, 9)
PI_4 = float(np.float32(TWO_PI - PI_1 - PI_2 - PI_3))
ROUND = 1.5 * 2.0 ** 23
COARSE = 256.0
PI_LOW = float(np.nextafter(np.float32(np.pi), np.float32(0)))

C_COND, C_LN1, C_LN2, C_FREQ = 0, KT * B, KT * B + KT, KT * B + 2 * KT
C_SMALL = C_FREQ + HALF
C_IDENT, C_MASK, C_SEL = 0, P, P + HEADS
C_CONST = C_SEL + 2 * P
CHUNKS = 1 + 3 * (IT // 2)
W_RING = 6
STACK = 3
KD = STACK * HD
QK_RING = 3
TAB_STEPS = 15
MROWS = 2 * 2 * HEADS


def block_program(nc, smalls, pos, x_t, tw1, tw2, wqkv, weights, consts, out_t):
    with ExitStack() as ctx:
        def sb(name, shape, dt=F32):
            return ctx.enter_context(nc.sbuf_tensor(name, shape, dt))

        def sem(name):
            return ctx.enter_context(nc.semaphore(name))

        small = sb("small", [P, C_SMALL])
        pos_i = sb("pos_i", [P, B], I32)
        const = sb("const", [P, C_CONST])
        x = sb("x", [P, KT, T])
        tw1_s = sb("tw1_s", [P, KT, D])
        tw2_s = sb("tw2_s", [P, KT, D])
        wqkv_s, wqkv_h, wqkv_l = (sb("wqkv_" + n, [P, KT, QKV], d) for n, d in (("s", F32), ("h", F32R), ("l", F32R)))
        w_s = sb("w_s", [P, W_RING, WIDE])
        w_h = sb("w_h", [P, CHUNKS, WIDE], F32R)
        w_l = sb("w_l", [P, CHUNKS, WIDE], F32R)
        ones = sb("ones", [P, P])
        eps = sb("eps", [P, 1])
        sel = sb("sel", [MROWS, 2, P], F32R)
        gain1 = sb("gain1", [P, KT, B])
        gain2 = sb("gain2", [P, KT, B])
        norm = sb("norm", [P, KT, HT])
        norm_h = sb("norm_h", [P, KT, T], F32R)
        norm_l = sb("norm_l", [P, KT, T], F32R)
        square = sb("square", [P, KT, HT])
        square_sum = sb("square_sum", [P, T])
        angle = sb("angle", [P, B, HALF])
        turns = sb("turns", [P, B, HALF])
        wrap = sb("wrap", [P, 2, B, HALF])
        trig = sb("trig", [P, 2, B, HALF])
        rope_c = sb("rope_c", [P, B, 2, HALF])
        rope_s = sb("rope_s", [P, B, 2, HALF])
        rms_ln = sb("rms_ln", [P, B])
        rstd1 = sb("rstd1", [P, B])
        by_cos = sb("by_cos", [P, NR, HD])
        by_sin = sb("by_sin", [P, NR, HD])
        turned = sb("turned", [P, 2, NR, HD])
        parts = sb("parts", [P, 2, NR, STACK, HD], F32R)
        v = sb("v", [P, B, HD])
        q_t = sb("q_t", [KD, QK_RING, HEADS, S], F32R)
        k_t = sb("k_t", [KD, QK_RING, S], F32R)
        top = sb("top", [P, 2, 2, HEADS])
        top_parts = sb("top_parts", [P, 2, 2, 2, HEADS], F32R)
        top_t = sb("top_t", [MROWS, 2, S])
        top_rows = sb("top_rows", [MROWS, 2, HEADS, S], F32R)
        prob = sb("prob", [P, 2, HEADS, S])
        sum_ln = sb("sum_ln", [P, KT * S])
        sum_inv = sb("sum_inv", [P, 2, KT * S])
        ctx_n = sb("ctx_n", [P, 2, KT, S])
        ctx_h = sb("ctx_h", [P, KT, T], F32R)
        ctx_l = sb("ctx_l", [P, KT, T], F32R)
        rstd2 = sb("rstd2", [P, HT])
        gate = sb("gate", [P, 2, WIDE])
        act = sb("act", [P, 2, WIDE])
        act_h = sb("act_h", [P, 3, WIDE], F32R)
        act_l = sb("act_l", [P, 3, WIDE], F32R)

        def bank(name):
            return ctx.enter_context(nc.psum_tensor(name, [P, WIDE], F32))

        a_ring = [bank(f"a_ring{i}") for i in range(2)]
        v_ring = [bank(f"v_ring{i}") for i in range(2)]
        s_ring = [bank(f"s_ring{i}") for i in range(2)]
        qkv_bank = bank("qkv_bank")
        pv_bank = bank("pv_bank")

        ld_small, ld_pos, ld_tw1, ld_tw2 = sem("ld_small"), sem("ld_pos"), sem("ld_tw1"), sem("ld_tw2")
        ld_x = [sem(f"ld_x{i}") for i in range(2)]
        ld_wqkv, ld_const = sem("ld_wqkv"), sem("ld_const")
        ld_w = [sem(f"ld_w{i}") for i in range(W_RING)]
        ones_ready, eps_ready, sel_ready = sem("ones_ready"), sem("eps_ready"), sem("sel_ready")
        scale1_done, scale2_done, gain1_ready, gain2_ready = sem("scale1_done"), sem("scale2_done"), sem("gain1_ready"), sem("gain2_ready")
        tab_step = sem("tab_step")
        trig_ready, table_ready = sem("trig_ready"), sem("table_ready")
        sq_ready, sqsum_ready, ss_done, ln1_ready, rstd1_ready = sem("sq_ready"), sem("sqsum_ready"), sem("ss_done"), sem("ln1_ready"), sem("rstd1_ready")
        xg_ready, xh_ready, xl_ready = sem("xg_ready"), sem("xh_ready"), sem("xl_ready")
        xl_late_ready = sem("xl_late_ready")
        wqkvh_ready, wqkvl_ready = sem("wqkvh_ready"), sem("wqkvl_ready")
        wh_ready, wl_ready = sem("wh_ready"), sem("wl_ready")
        qkv_done, qkv_read = sem("qkv_done"), sem("qkv_read")
        rope_step = sem("rope_step")
        turned_ready, hi_ready, lo_ready = sem("turned_ready"), sem("hi_ready"), sem("lo_ready")
        a_full, a_free = sem("a_full"), sem("a_free")
        v_full, v_free = sem("v_full"), sem("v_free")
        top_hi, top_ready, rows_ready, top_t_ready = sem("top_hi"), sem("top_ready"), sem("rows_ready"), sem("top_t_ready")
        s_full, s_free = sem("s_full"), sem("s_free")
        pv_done, sumln_ready, suminv_ready, ctxn_ready, ctxh_ready, ctxl_ready = (
            sem("pv_done"), sem("sumln_ready"), sem("suminv_ready"), sem("ctxn_ready"), sem("ctxh_ready"), sem("ctxl_ready"))
        sq2_ready, sq2sum_ready, rstd2_ready = sem("sq2_ready"), sem("sq2sum_ready"), sem("rstd2_ready")
        h2_ready, h2h_ready, h2l_ready = sem("h2_ready"), sem("h2h_ready"), sem("h2l_ready")
        acth_ready, actl_ready = sem("acth_ready"), sem("actl_ready")
        down_done = sem("down_done")
        y_ready, stored = sem("y_ready"), sem("stored")

        ident = const[:, C_IDENT:C_IDENT + P]

        def toks(b, n=1):
            return slice(b * S, (b + n) * S)

        def half(h):
            return slice(h * HT, (h + 1) * HT)

        def gate_chunk(i):
            return 1 + 3 * (i // 2)

        A_ORDER, V_ORDER = [], []
        for s in range(B + 1):
            if s < B:
                A_ORDER += [("k", s), ("q", s, 0), ("q", s, 1)]
            if s % 2 == 0 and s >= 2:
                A_ORDER.append(("top", s // 2 - 1))
            if s < B:
                V_ORDER += [("s1", s, 0), ("s1", s, 1)]
            if s == 6:
                V_ORDER += [("wo", 0, 0), ("wo", 0, 1)]
        A_ORDER.append(("ss", 0))
        for i in range(IT):
            A_ORDER.append(("g", 0, i))
            V_ORDER.append(("u", 0, i))
            if i == 1:
                V_ORDER += [("wo", 1, 0), ("wo", 1, 1)]
            if i == 3:
                A_ORDER.append(("ss", 1))
        for i in range(IT):
            A_ORDER.append(("g", 1, i))
            V_ORDER.append(("u", 1, i))
        A_AT = {k: n for n, k in enumerate(A_ORDER)}
        V_AT = {k: n for n, k in enumerate(V_ORDER)}

        block = ctx.enter_context(nc.Block())

        @block.sync
        def _(sp):
            sp.dma_start(small[:, :], smalls).then_inc(ld_small, 16)
            sp.dma_start(tw1_s[:, :, :], tw1.rearrange("(k p) n -> p k n", p=P)).then_inc(ld_tw1, 16)
            xd = x_t.rearrange("(k p) n -> p k n", p=P)
            sp.dma_start(x[:, :, half(0)], xd[:, :, half(0)]).then_inc(ld_x[0], 16)
            sp.dma_start(wqkv_s[:, :, :], wqkv.rearrange("(k p) n -> p k n", p=P)).then_inc(ld_wqkv, 16)
            sp.dma_start(x[:, :, half(1)], xd[:, :, half(1)]).then_inc(ld_x[1], 16)
            sp.dma_start(const[:, :], consts).then_inc(ld_const, 16)
            sp.dma_start(tw2_s[:, :, :], tw2.rearrange("(k p) n -> p k n", p=P)).then_inc(ld_tw2, 16)
            for n in range(CHUNKS):
                if n >= W_RING:
                    sp.wait_ge(wl_ready, n - W_RING + 1)
                sp.dma_start(w_s[:, n % W_RING, :], weights[:, n, :]).then_inc(ld_w[n % W_RING], 16)
            od = out_t.rearrange("(k p) n -> p k n", p=P)
            for h in range(2):
                for m in range(KT):
                    sp.wait_ge(y_ready, KT * h + m + 1)
                    sp.dma_start(od[:, m, half(h)], x[:, m, half(h)]).then_inc(stored, 16)
            sp.wait_ge(stored, 16 * 2 * KT)

        @block.tensor
        def _(pe):
            def a_slot(key):
                n = A_AT[key]
                if n >= 2:
                    pe.wait_ge(a_free, n - 1)
                return a_ring[n % 2]

            def v_slot(key):
                n = V_AT[key]
                if n >= 2:
                    pe.wait_ge(v_free, n - 1)
                return v_ring[n % 2]

            def three_pass(dst, pairs, first=True, last=True):
                terms = [t for wh, wl, xh, xl in pairs for t in ((wh, xh), (wh, xl), (wl, xh))]
                for n, (w, d) in enumerate(terms):
                    mm = pe.matmul(dst, w, d, start=first and n == 0, stop=last and n == len(terms) - 1)
                return mm

            def scales(tw, ld, dst, done):
                pe.wait_ge(ld, 16)
                for m in range(KT):
                    for k in range(KT):
                        mm = pe.matmul(dst[:, m * B:(m + 1) * B], tw[:, k, m * P:(m + 1) * P],
                                       small[:, C_COND + k * B:C_COND + (k + 1) * B], start=k == 0, stop=k == KT - 1)
                mm.then_inc(done, 1)

            def project(b):
                pe.wait_ge(xh_ready, b // 2 + 1)
                if b < HB:
                    pe.wait_ge(xl_ready, b // 2 + 1)
                else:
                    pe.wait_ge(xl_late_ready, b // 2 - 1)
                if b >= 1:
                    pe.wait_ge(qkv_read, b)
                dst = qkv_bank[:, 0:QKV]
                terms = [t for k in range(KT) for t in (
                    (norm_h[:, k, toks(b)], wqkv_h[:, k, :]), (norm_l[:, k, toks(b)], wqkv_h[:, k, :]),
                    (norm_h[:, k, toks(b)], wqkv_l[:, k, :]))]
                for n, (w, d) in enumerate(terms):
                    mm = pe.matmul(dst, w, d, start=n == 0, stop=n == len(terms) - 1)
                mm.then_inc(qkv_done, 1)

            def turn(b):
                pe.wait_ge(hi_ready, 2 * (b + 1))
                pe.wait_ge(lo_ready, 2 * (b + 1))
                src = parts[:, b % 2, :, :, :].rearrange("p h a d -> p h (a d)").bitcast(F32)
                dst = a_slot(("k", b))
                pe.transpose(dst[0:KD, 0:S], src[:, HEADS, :], ident).then_inc(a_full, 1)
                for g in range(2):
                    dst = a_slot(("q", b, g))
                    for j in range(4):
                        mm = pe.transpose(dst[0:KD, j * S:(j + 1) * S], src[:, 4 * g + j, :], ident)
                    mm.then_inc(a_full, 1)

            def scores(b):
                for g in range(2):
                    pe.wait_ge(a_free, A_AT[("q", b, g)] + 1)
                    dst = v_slot(("s1", b, g))
                    for j in range(4):
                        mm = pe.matmul(dst[:, j * S:(j + 1) * S], q_t[:, b % QK_RING, 4 * g + j, :], k_t[:, b % QK_RING, :],
                                       start=True, stop=True)
                    mm.then_inc(v_full, 1)

            def turn_top(p):
                pe.wait_ge(top_ready, p + 1)
                dst = a_slot(("top", p))
                pe.transpose(dst[0:MROWS, 0:S],
                             top_parts[:, p % 2, :, :, :].rearrange("p a b h -> p (a b h)").bitcast(F32),
                             ident).then_inc(a_full, 1)

            def scores_t(b):
                pe.wait_ge(rows_ready, b // 2 + 1)
                for g in range(2):
                    n = 2 * b + g
                    if n >= 2:
                        pe.wait_ge(s_free, n - 1)
                    dst = s_ring[n % 2][:, :]
                    heads = slice(4 * g, 4 * g + 4)
                    pe.matmul(dst, k_t[:, b % QK_RING, :], q_t[:, b % QK_RING, heads, :].rearrange("p h t -> p (h t)"),
                              start=True, stop=False)
                    pe.matmul(dst, sel[:, b % 2, :], top_rows[:, b // 2 % 2, heads, :].rearrange("p h t -> p (h t)"),
                              start=False, stop=True).then_inc(s_full, 1)

            def values(b):
                pe.wait_ge(s_free, 2 * b + 2)
                if b >= 1:
                    pe.wait_ge(ctxn_ready, b)
                for n, w in enumerate((v[:, b, :], ones[:, 0:HD])):
                    for t in range(KT):
                        for j in range(4):
                            at = n * KT * S + t * S
                            mm = pe.matmul(pv_bank[HD * j:HD * (j + 1), at:at + S], w, prob[:, b % 2, 4 * t + j, :],
                                           start=True, stop=True, tile_position=(0, HD * j))
                mm.then_inc(pv_done, 1)

            def out_project(h):
                pe.wait_ge(wl_ready, 1)
                pe.wait_ge(ctxh_ready, HB * (h + 1))
                pe.wait_ge(ctxl_ready, HB * (h + 1))
                for m in range(KT):
                    dst = v_slot(("wo", h, m))
                    three_pass(dst[:, :], [(w_h[:, 0, k * D + m * P:k * D + (m + 1) * P], w_l[:, 0, k * D + m * P:k * D + (m + 1) * P], ctx_h[:, k, half(h)], ctx_l[:, k, half(h)])
                                           for k in range(KT)]).then_inc(v_full, 1)

            def sum_squares(h):
                pe.wait_ge(sq2sum_ready, h + 1)
                dst = a_slot(("ss", h))
                pe.matmul(dst[:, :], ones[:, :], square_sum[:, half(h)], start=True, stop=True).then_inc(a_full, 1)

            def gate_up(h, i):
                if i == 0:
                    pe.wait_ge(h2h_ready, KT * (h + 1))
                    pe.wait_ge(h2l_ready, KT * (h + 1))
                pe.wait_ge(wl_ready, gate_chunk(i) + 2)
                for slot, key, n, full in ((a_slot, "g", gate_chunk(i), a_full), (v_slot, "u", gate_chunk(i) + 1, v_full)):
                    dst = slot((key, h, i))
                    cols = [slice(k * 2 * P + i % 2 * P, k * 2 * P + i % 2 * P + P) for k in range(KT)]
                    three_pass(dst[:, :], [(w_h[:, n, cols[k]], w_l[:, n, cols[k]], norm_h[:, k, half(h)], norm_l[:, k, half(h)])
                                           for k in range(KT)]).then_inc(full, 1)

            def down(h, i):
                n = h * IT + i
                chunk = gate_chunk(i) + 2
                pe.wait_ge(wl_ready, chunk + 1)
                pe.wait_ge(actl_ready, n + 1)
                if i == 0 and h == 0:
                    pe.wait_ge(s_free, 2 * B)
                if i == 0 and h == 1:
                    pe.wait_ge(y_ready, KT)
                for m in range(KT):
                    r = slice(i % 2 * D + m * P, i % 2 * D + (m + 1) * P)
                    mm = three_pass(s_ring[m][:, :], [(w_h[:, chunk, r], w_l[:, chunk, r], act_h[:, n % 3, :], act_l[:, n % 3, :])],
                                    first=i == 0, last=i == IT - 1)
                mm.then_inc(down_done, 1)

            pe.wait_ge(ld_small, 16)
            scales(tw1_s, ld_tw1, pv_bank, scale1_done)
            pe.wait_ge(wqkvh_ready, 1)
            pe.wait_ge(wqkvl_ready, 1)
            project(0)
            pe.wait_ge(ones_ready, 1)
            pe.wait_ge(sqsum_ready, 2)
            pe.wait_ge(gain1_ready, KT)
            for b in range(B):
                mm = pe.matmul(pv_bank[:, b:b + 1], square_sum[:, toks(b)], ones[:, 0:1], start=True, stop=True)
            mm.then_inc(ss_done, 1)
            pe.wait_ge(ld_const, 16)
            for s in range(B + 3):
                if s < B:
                    turn(s)
                if s == 0:
                    project(1)
                if s == 1:
                    pe.wait_ge(ln1_ready, 1)
                    scales(tw2_s, ld_tw2, pv_bank, scale2_done)
                    pe.wait_ge(gain2_ready, KT)
                if s % 2 == 0 and 2 <= s:
                    if s <= B:
                        turn_top(s // 2 - 1)
                    if s >= 4:
                        values(s - 3)
                if s % 2 == 1 and s >= 3:
                    scores_t(s - 2)
                    values(s - 3)
                if s < B:
                    if s == 3:
                        pe.wait_ge(sel_ready, 1)
                    scores(s)
                if s + 2 < B:
                    project(s + 2)
                if s % 2 == 0 and 2 <= s <= B:
                    if s == 2:
                        pe.wait_ge(sel_ready, 1)
                    scores_t(s - 2)
                if s == 6:
                    out_project(0)
            sum_squares(0)
            for h in range(2):
                for i in range(IT):
                    gate_up(h, i)
                    if i >= 2:
                        down(h, i - 2)
                    if h == 0 and i == 1:
                        out_project(1)
                    if h == 0 and i == 3:
                        sum_squares(1)
                down(h, IT - 2)
                down(h, IT - 1)

        @block.scalar
        def _(act_e):
            act_e.dma_start(pos_i[:, :], pos).then_inc(ld_pos, 16)

            def copy(dst, src):
                return nc.scalar.activation(dst, src, ACT.Copy)

            def cut_x(p):
                act_e.wait_ge(xg_ready, p + 1)
                copy(norm_h[:, :, toks(2 * p, 2)], norm[:, :, toks(2 * (p % 2), 2)]).then_inc(xh_ready, 1)

            def square_x(h):
                act_e.wait_ge(ld_x[h], 16)
                if h:
                    act_e.wait_ge(sqsum_ready, h)
                nc.scalar.activation(square[:, :, :], x[:, :, half(h)], ACT.Square).then_inc(sq_ready, 1)

            def cut_weight(n):
                act_e.wait_ge(ld_w[n % W_RING], 16 * (n // W_RING + 1))
                copy(w_h[:, n, :], w_s[:, n % W_RING, :]).then_inc(wh_ready, 1)

            def take(key):
                n = A_AT[key]
                act_e.wait_ge(a_full, n + 1)
                return a_ring[n % 2]

            def take_turned(b):
                if b >= QK_RING:
                    act_e.wait_ge(s_full, 2 * (b - QK_RING) + 2)
                src = take(("k", b))
                copy(k_t[:, b % QK_RING, :], src[0:KD, 0:S]).then_inc(a_free, 1)
                for g in range(2):
                    src = take(("q", b, g))
                    copy(q_t[:, b % QK_RING, 4 * g:4 * g + 4, :], src[0:KD, :].rearrange("p (h t) -> p h t", h=4)).then_inc(a_free, 1)

            def take_top(p):
                src = take(("top", p))
                if p >= 2:
                    act_e.wait_ge(rows_ready, p - 1)
                nc.scalar.activation(top_t[:, p % 2, :], src[0:MROWS, 0:S], ACT.Copy).then_inc(a_free, 1)

            def exps(b):
                if b >= 2:
                    act_e.wait_ge(pv_done, b - 1)
                for g in range(2):
                    n = 2 * b + g
                    act_e.wait_ge(s_full, n + 1)
                    nc.scalar.activation(prob[:, b % 2, 4 * g:4 * g + 4, :], s_ring[n % 2][:, :].rearrange("p (h t) -> p h t", h=4),
                                         ACT.Exp, scale=SCALE).then_inc(s_free, 1)

            def invert_sums(b):
                act_e.wait_ge(pv_done, b + 1)
                if b >= 1:
                    act_e.wait_ge(suminv_ready, b)
                nc.scalar.activation(sum_ln[:, :], pv_bank[:, KT * S:2 * KT * S], ACT.Ln).then_inc(sumln_ready, 1)
                act_e.wait_ge(sumln_ready, b + 1)
                if b >= 2:
                    act_e.wait_ge(ctxn_ready, b - 1)
                nc.scalar.activation(sum_inv[:, b % 2, :], sum_ln[:, :], ACT.Exp, scale=-1.0).then_inc(suminv_ready, 1)

            def cut_ctx(b):
                act_e.wait_ge(ctxn_ready, b + 1)
                copy(ctx_h[:, :, toks(b)], ctx_n[:, b % 2, :, :]).then_inc(ctxh_ready, 1)

            def square_x2(h):
                for m in range(KT):
                    act_e.wait_ge(v_free, V_AT[("wo", h, m)] + 1)
                    if h:
                        act_e.wait_ge(sq2sum_ready, h)
                    nc.scalar.activation(square[:, m, :], x[:, m, half(h)], ACT.Square).then_inc(sq2_ready, 1)

            def root2(h):
                src = take(("ss", h))
                if h:
                    act_e.wait_ge(h2_ready, KT * h)
                nc.scalar.activation(rstd2[:, :], src[:, :], ACT.Ln, scale=1.0 / D, bias=eps[:, 0:1]).then_inc(a_free, 1)
                act_e.wait_ge(a_free, A_AT[("ss", h)] + 1)
                nc.scalar.activation(rstd2[:, :], rstd2[:, :], ACT.Exp, scale=-0.5).then_inc(rstd2_ready, 1)

            def cut_h2(h):
                for k in range(KT):
                    act_e.wait_ge(h2_ready, KT * h + k + 1)
                    copy(norm_h[:, k, half(h)], norm[:, k, :]).then_inc(h2h_ready, 1)

            def silu(h, i):
                n = h * IT + i
                src = take(("g", h, i))
                if n >= 2:
                    act_e.wait_ge(v_free, V_AT[("u",) + divmod(n - 2, IT)] + 1)
                nc.scalar.activation(gate[:, n % 2, :], src[:, :], ACT.Silu).then_inc(a_free, 1)

            act_e.wait_ge(tab_step, TAB_STEPS)
            nc.scalar.activation(trig[:, :, :, :], wrap[:, :, :, :], ACT.Sin).then_inc(trig_ready, 1)
            nc.scalar.preload_act_table_set("natural_log_exp_and_others")
            cut_x(0)
            act_e.wait_ge(ld_wqkv, 16)
            copy(wqkv_h[:, :, :], wqkv_s[:, :, :]).then_inc(wqkvh_ready, 1)
            square_x(0)
            cut_x(1)
            square_x(1)
            act_e.wait_ge(ss_done, 1)
            act_e.wait_ge(eps_ready, 1)
            nc.scalar.activation(rms_ln[:, :], pv_bank[:, 0:B], ACT.Ln, scale=1.0 / D, bias=eps[:, 0:1]).then_inc(ln1_ready, 1)
            act_e.wait_ge(ln1_ready, 1)
            nc.scalar.activation(rstd1[:, :], rms_ln[:, :], ACT.Exp, scale=-0.5).then_inc(rstd1_ready, 1)
            cut_x(2)
            cut_x(3)
            act_e.wait_ge(ld_const, 16)
            copy(sel[:, :, :], const[0:MROWS, C_SEL:C_SEL + 2 * P].rearrange("p (b n) -> p b n", b=2)).then_inc(sel_ready, 1)
            chunk = 0
            for s in range(B + 3):
                if s < B:
                    take_turned(s)
                if s % 2 == 0 and 2 <= s:
                    if s <= B:
                        take_top(s // 2 - 1)
                    if s >= 4:
                        invert_sums(s - 3)
                        cut_ctx(s - 3)
                    if s <= B:
                        exps(s - 2)
                if s % 2 == 1 and s >= 3:
                    exps(s - 2)
                    invert_sums(s - 3)
                    cut_ctx(s - 3)
                for _ in range(2):
                    if chunk < CHUNKS:
                        cut_weight(chunk)
                        chunk += 1
                if s == 7:
                    square_x2(0)
            assert chunk == CHUNKS
            root2(0)
            cut_h2(0)
            for i in range(IT):
                silu(0, i)
                if i == 2:
                    square_x2(1)
                if i == 3:
                    root2(1)
                if i == 4:
                    cut_h2(1)
            for i in range(IT):
                silu(1, i)

        @block.vector
        def _(dve):
            ve = nc.vector
            table = [0]

            def tab(ins):
                table[0] += 1
                ins.then_inc(tab_step, 1)
                dve.wait_ge(tab_step, table[0])

            def reduce_turns(count_scale, unit):
                tab(ve.tensor_scalar(turns[:, :, :], angle[:, :, :], count_scale, ROUND, ALU.mult, ALU.add))
                tab(ve.tensor_scalar(turns[:, :, :], turns[:, :, :], -ROUND, None, ALU.add))
                for part in (PI_1, PI_2, PI_3, PI_4):
                    tab(ve.scalar_tensor_tensor(out=angle[:, :, :], in0=turns[:, :, :], scalar=-part * unit,
                                                in1=angle[:, :, :], op0=ALU.mult, op1=ALU.add))

            def gain(scale, c_ln, dst, done, ready):
                dve.wait_ge(done, 1)
                for k in range(KT):
                    ve.tensor_scalar(dst[:, k, :], scale[:, k * B:(k + 1) * B], 1.0, small[:, c_ln + k:c_ln + k + 1],
                                     ALU.add, ALU.mult).then_inc(ready, 1)

            def gain_x(p):
                r = toks(2 * p, 2)
                dve.wait_ge(ld_x[p // 2], 16)
                dve.wait_ge(gain1_ready, KT)
                if p >= 2:
                    dve.wait_ge(xh_ready, p - 1)
                    dve.wait_ge(xl_ready, p - 1)
                ve.tensor_tensor(norm[:, :, toks(2 * (p % 2), 2)].rearrange("p k (b t) -> p k b t", b=2),
                                 x[:, :, r].rearrange("p k (b t) -> p k b t", b=2),
                                 gain1[:, :, 2 * p:2 * p + 2].unsqueeze(3).to_broadcast([P, KT, 2, S]),
                                 ALU.mult).then_inc(xg_ready, 1)

            def rest_x(p):
                r = toks(2 * p, 2)
                dve.wait_ge(xh_ready, p + 1)
                ve.tensor_tensor(norm_l[:, :, r], norm[:, :, toks(2 * (p % 2), 2)], norm_h[:, :, r].bitcast(F32), ALU.subtract).then_inc(xl_ready, 1)

            def rotate(b):
                s = b % 2
                dve.wait_ge(qkv_done, b + 1)
                if b == 0:
                    dve.wait_ge(table_ready, 3)
                if b >= 2:
                    dve.wait_ge(lo_ready, 2 * (b - 1))
                    dve.wait_ge(a_full, A_AT[("q", b - 2, 1)] + 1)
                src = qkv_bank[:, 0:NR * HD].rearrange("p (h a d) -> p h a d", h=NR, a=2)
                ve.tensor_tensor(by_cos[:, :, :], qkv_bank[:, 0:NR * HD].rearrange("p (h d) -> p h d", h=NR),
                                 rope_c[:, b, :, :].rearrange("p a d -> p (a d)").unsqueeze(1).to_broadcast([P, NR, HD]),
                                 ALU.mult).then_inc(rope_step, 1)
                for a in range(2):
                    ve.tensor_tensor(by_sin[:, :, :].rearrange("p h (a d) -> p h a d", a=2)[:, :, a, :], src[:, :, 1 - a, :],
                                     rope_s[:, b, a, :].unsqueeze(1).to_broadcast([P, NR, HALF]),
                                     ALU.mult).then_inc(rope_step, 1)
                ve.tensor_scalar(v[:, b, :], qkv_bank[:, NR * HD:QKV], rstd1[:, b:b + 1], None, ALU.mult).then_inc(qkv_read, 1)
                dve.wait_ge(rope_step, 3 * (b + 1))
                ve.tensor_tensor(turned[:, s, :, :], by_cos[:, :, :], by_sin[:, :, :], ALU.add).then_inc(turned_ready, 1)
                dve.wait_ge(turned_ready, b + 1)
                ve.tensor_copy(parts[:, s, 0:HEADS, 0:STACK:2, :],
                               turned[:, s, 0:HEADS, :].unsqueeze(2).to_broadcast([P, HEADS, 2, HD])).then_inc(hi_ready, 1)
                ve.tensor_copy(parts[:, s, HEADS, 0:2, :],
                               turned[:, s, HEADS, :].unsqueeze(1).to_broadcast([P, 2, HD])).then_inc(hi_ready, 1)

            def maxima(b):
                for g in range(2):
                    n = V_AT[("s1", b, g)]
                    dve.wait_ge(v_full, n + 1)
                    if g == 0 and b >= 4:
                        dve.wait_ge(top_ready, b // 2 - 1)
                    ve.tensor_reduce(top[:, b // 2 % 2, b % 2, 4 * g:4 * g + 4],
                                     v_ring[n % 2][:, :].rearrange("p (h k) -> p h k", h=4), AX.X, ALU.max).then_inc(v_free, 1)
                if b % 2:
                    p = b // 2
                    dve.wait_ge(v_free, V_AT[("s1", b, 1)] + 1)
                    if p >= 2:
                        dve.wait_ge(a_full, A_AT[("top", p - 2)] + 1)
                    ve.tensor_copy(top_parts[:, p % 2, 0, :, :], top[:, p % 2, :, :]).then_inc(top_hi, 1)
                    dve.wait_ge(top_hi, p + 1)
                    ve.tensor_tensor(top_parts[:, p % 2, 1, :, :], top[:, p % 2, :, :],
                                     top_parts[:, p % 2, 0, :, :].bitcast(F32), ALU.subtract).then_inc(top_ready, 1)

            def norm_ctx(b):
                dve.wait_ge(suminv_ready, b + 1)
                if b >= 2:
                    dve.wait_ge(ctxh_ready, b - 1)
                    dve.wait_ge(ctxl_ready, b - 1)
                ve.tensor_tensor(ctx_n[:, b % 2, :, :].rearrange("p k t -> p (k t)"), pv_bank[:, 0:KT * S],
                                 sum_inv[:, b % 2, :], ALU.mult).then_inc(ctxn_ready, 1)

            def residual1(h):
                for m in range(KT):
                    n = V_AT[("wo", h, m)]
                    dve.wait_ge(v_full, n + 1)
                    ve.tensor_tensor(x[:, m, half(h)], v_ring[n % 2][:, :], x[:, m, half(h)], ALU.add).then_inc(v_free, 1)

            def add_squares2(h):
                dve.wait_ge(sq2_ready, KT * (h + 1))
                ve.tensor_tensor(square_sum[:, half(h)], square[:, 0, :], square[:, 1, :], ALU.add).then_inc(sq2sum_ready, 1)

            def scale_h2(h):
                dve.wait_ge(rstd2_ready, h + 1)
                if h == 0:
                    dve.wait_ge(xl_late_ready, 2)
                for k in range(KT):
                    for b in range(HB * h, HB * (h + 1)):
                        ins = ve.scalar_tensor_tensor(out=norm[:, k, toks(b - HB * h)], in0=x[:, k, toks(b)], scalar=gain2[:, k, b:b + 1],
                                                      in1=rstd2[:, toks(b - HB * h)], op0=ALU.mult, op1=ALU.mult)
                    ins.then_inc(h2_ready, 1)
                for k in range(KT):
                    dve.wait_ge(h2h_ready, KT * h + k + 1)
                    ve.tensor_tensor(norm_l[:, k, half(h)], norm[:, k, :], norm_h[:, k, half(h)].bitcast(F32),
                                     ALU.subtract).then_inc(h2l_ready, 1)

            def activate(h, i):
                n = h * IT + i
                at = V_AT[("u", h, i)]
                dve.wait_ge(v_full, at + 1)
                dve.wait_ge(a_free, A_AT[("g", h, i)] + 1)
                if n >= 3:
                    dve.wait_ge(down_done, n - 2)
                ve.tensor_tensor(act[:, n % 2, :], v_ring[at % 2][:, :], gate[:, n % 2, :], ALU.mult).then_inc(v_free, 1)
                dve.wait_ge(v_free, at + 1)
                ve.tensor_copy(act_h[:, n % 3, :], act[:, n % 2, :]).then_inc(acth_ready, 1)
                dve.wait_ge(acth_ready, n + 1)
                ve.tensor_tensor(act_l[:, n % 3, :], act[:, n % 2, :], act_h[:, n % 3, :].bitcast(F32),
                                 ALU.subtract).then_inc(actl_ready, 1)

            def residual2(h):
                dve.wait_ge(down_done, IT * (h + 1))
                for m in range(KT):
                    ve.tensor_tensor(x[:, m, half(h)], s_ring[m][:, :], x[:, m, half(h)], ALU.add).then_inc(y_ready, 1)

            ve.memset(eps[:, :], EPS).then_inc(eps_ready, 1)
            dve.wait_ge(ld_pos, 16)
            dve.wait_ge(ld_small, 16)
            tab(ve.tensor_tensor(angle[:, :, :], pos_i[:, :].unsqueeze(2).to_broadcast([P, B, HALF]),
                                 small[:, C_FREQ:C_FREQ + HALF].unsqueeze(1).to_broadcast([P, B, HALF]), ALU.mult))
            reduce_turns(1.0 / (TWO_PI * COARSE), COARSE)
            reduce_turns(1.0 / TWO_PI, 1.0)
            tab(ve.tensor_scalar(wrap[:, 0, :, :], angle[:, :, :], PI_LOW, -PI_LOW, ALU.min, ALU.max))
            ve.tensor_scalar(turns[:, :, :], angle[:, :, :], float(np.pi / 2), -TWO_PI, ALU.is_gt, ALU.mult).then_inc(table_ready, 1)
            dve.wait_ge(table_ready, 1)
            ve.scalar_tensor_tensor(out=angle[:, :, :], in0=angle[:, :, :], scalar=float(np.pi / 2), in1=turns[:, :, :],
                                    op0=ALU.add, op1=ALU.add).then_inc(table_ready, 1)
            dve.wait_ge(table_ready, 2)
            tab(ve.tensor_scalar(wrap[:, 1, :, :], angle[:, :, :], PI_LOW, -PI_LOW, ALU.min, ALU.max))
            assert table[0] == TAB_STEPS

            gain(pv_bank, C_LN1, gain1, scale1_done, gain1_ready)
            gain_x(0)
            gain_x(1)
            rest_x(0)
            rest_x(1)
            gain_x(2)
            gain_x(3)
            dve.wait_ge(trig_ready, 1)
            dve.wait_ge(rstd1_ready, 1)
            rs = rstd1[:, :].unsqueeze(2).to_broadcast([P, B, HALF])
            for a in range(2):
                ve.tensor_tensor(rope_c[:, :, a, :], trig[:, 1, :, :], rs, ALU.mult)
            ve.tensor_tensor(rope_s[:, :, 1, :], trig[:, 0, :, :], rs, ALU.mult).then_inc(table_ready, 1)
            dve.wait_ge(table_ready, 3)
            ve.tensor_scalar(rope_s[:, :, 0, :], rope_s[:, :, 1, :], -1.0, None, ALU.mult).then_inc(table_ready, 1)
            dve.wait_ge(table_ready, 4)
            rotate(0)
            for s in range(B + 3):
                if s + 1 < B:
                    rotate(s + 1)
                if s == 1:
                    gain(pv_bank, C_LN2, gain2, scale2_done, gain2_ready)
                if s >= 3 and s - 3 < B:
                    norm_ctx(s - 3)
                if s < B:
                    maxima(s)
                if s == 6:
                    residual1(0)
                if s == 7:
                    add_squares2(0)
            scale_h2(0)
            for h in range(2):
                for i in range(IT):
                    activate(h, i)
                    if h == 0 and i == 1:
                        residual1(1)
                    if h == 0 and i == 2:
                        add_squares2(1)
                    if h == 0 and i == 3:
                        scale_h2(1)
                residual2(h)

        @block.gpsimd
        def _(pool):
            gp = nc.gpsimd
            gp.memset(ones[:, :], 1.0).then_inc(ones_ready, 1)

            def rest_weight(n):
                pool.wait_ge(wh_ready, n + 1)
                gp.tensor_tensor(w_l[:, n, :], w_s[:, n % W_RING, :], w_h[:, n, :].bitcast(F32), ALU.subtract).then_inc(wl_ready, 1)

            def add_squares(h):
                pool.wait_ge(sq_ready, h + 1)
                gp.tensor_tensor(square_sum[:, half(h)], square[:, 0, :], square[:, 1, :], ALU.add).then_inc(sqsum_ready, 1)

            def rest_x(p):
                r = toks(2 * p, 2)
                pool.wait_ge(xh_ready, p + 1)
                gp.tensor_tensor(norm_l[:, :, r], norm[:, :, toks(2 * (p % 2), 2)], norm_h[:, :, r].bitcast(F32), ALU.subtract).then_inc(xl_late_ready, 1)

            def rest_turned(b):
                pool.wait_ge(hi_ready, 2 * (b + 1))
                if b >= 2:
                    pool.wait_ge(a_full, A_AT[("q", b - 2, 1)] + 1)
                for heads, lo in ((slice(0, HEADS), 1), (slice(HEADS, NR), 2)):
                    gp.tensor_tensor(parts[:, b % 2, heads, lo, :], turned[:, b % 2, heads, :],
                                     parts[:, b % 2, heads, 0, :].bitcast(F32), ALU.subtract).then_inc(lo_ready, 1)

            def spread_top(p):
                pool.wait_ge(a_free, A_AT[("top", p)] + 1)
                if p >= 2:
                    pool.wait_ge(s_full, 4 * (p - 1))
                gp.tensor_tensor(top_rows[:, p % 2, :, :], top_t[:, p % 2, :].unsqueeze(1).to_broadcast([MROWS, HEADS, S]),
                                 const[0:MROWS, C_MASK:C_MASK + HEADS].unsqueeze(2).to_broadcast([MROWS, HEADS, S]),
                                 ALU.mult).then_inc(rows_ready, 1)

            def rest_ctx(b):
                pool.wait_ge(ctxh_ready, b + 1)
                gp.tensor_tensor(ctx_l[:, :, toks(b)], ctx_n[:, b % 2, :, :], ctx_h[:, :, toks(b)].bitcast(F32),
                                 ALU.subtract).then_inc(ctxl_ready, 1)

            pool.wait_ge(wqkvh_ready, 1)
            gp.tensor_tensor(wqkv_l[:, :, :], wqkv_s[:, :, :], wqkv_h[:, :, :].bitcast(F32), ALU.subtract).then_inc(wqkvl_ready, 1)
            add_squares(0)
            add_squares(1)
            rest_turned(0)
            rest_x(2)
            pool.wait_ge(ld_const, 16)
            chunk = 0
            for s in range(B + 3):
                if s + 1 < B:
                    rest_turned(s + 1)
                if s == 0:
                    rest_x(3)
                if s % 2 == 0 and 2 <= s <= B:
                    spread_top(s // 2 - 1)
                if s >= 3 and s - 3 < B:
                    rest_ctx(s - 3)
                for _ in range(2 if s >= 1 else 0):
                    if chunk < CHUNKS:
                        rest_weight(chunk)
                        chunk += 1
            while chunk < CHUNKS:
                rest_weight(chunk)
                chunk += 1


def kernel(x, pos_BxS, cond_2048, L0_cond_ln1_w, L0_cond_ln1_tw, L0_cond_ln2_w, L0_cond_ln2_tw,
           L0_cond_Wq, L0_cond_Wk, L0_cond_Wv, L0_cond_Wo, L0_cond_Wg, L0_cond_Wu, L0_cond_Wd):
    import concourse.bacc as _bacc
    from concourse import mybir as _mybir
    from concourse.bass_utils import run_bass_kernel_spmd as _run

    def rows(a):
        a = np.asarray(a)
        return a.reshape(KT, P, -1).transpose(1, 0, 2).reshape(P, -1)

    def turned(a):
        return np.ascontiguousarray(np.asarray(a).T)

    freq = (np.float32(1.0) / np.float32(ROPE_BASE) ** (np.arange(0, HD, 2, dtype=np.float32) / np.float32(HD))).astype(np.float32)
    const = np.zeros((P, C_CONST), np.float32)
    const[:, C_IDENT:C_IDENT + P] = np.eye(P, dtype=np.float32)
    for r in range(MROWS):
        const[r, C_MASK + r % HEADS] = -1.0
        b = r // HEADS % 2
        const[r, C_SEL + b * P:C_SEL + (b + 1) * P] = 1.0

    w_gate, w_up, w_down = rows(turned(L0_cond_Wg)), rows(turned(L0_cond_Wu)), np.asarray(L0_cond_Wd).T
    chunks = [rows(turned(L0_cond_Wo))]
    for c in range(IT // 2):
        for w in (w_gate, w_up):
            chunks.append(w.reshape(P, KT, INTER)[:, :, 2 * P * c:2 * P * (c + 1)].reshape(P, WIDE))
        chunks.append(w_down[2 * P * c:2 * P * (c + 1)].reshape(2, P, D).transpose(1, 0, 2).reshape(P, WIDE))
    arrays = {
        "smalls": np.concatenate([rows(turned(cond_2048)), rows(np.asarray(L0_cond_ln1_w)[:, None]),
                                  rows(np.asarray(L0_cond_ln2_w)[:, None]), np.broadcast_to(freq, (P, HALF))], axis=1),
        "pos": turned(pos_BxS),
        "x_t": turned(np.asarray(x).reshape(T, D)),
        "tw1": turned(L0_cond_ln1_tw),
        "tw2": turned(L0_cond_ln2_tw),
        "wqkv": np.concatenate([turned(L0_cond_Wq), turned(L0_cond_Wk), turned(L0_cond_Wv)], axis=1),
        "weights": np.stack(chunks, axis=1),
        "consts": const,
    }
    nc = _bacc.Bacc("TRN2", target_bir_lowering=False, num_devices=1)
    feeds, args = {}, []
    for name, a in arrays.items():
        a = np.ascontiguousarray(a)
        feeds[f"in_{name}"] = a
        args.append(nc.dram_tensor(f"in_{name}", a.shape, _mybir.dt.from_np(a.dtype), kind="ExternalInput").ap())
    out = nc.dram_tensor("out_t", (D, T), _mybir.dt.float32, kind="ExternalOutput").ap()
    block_program(nc, *args, out)
    r = _run(nc, [feeds], core_ids=[0])
    return np.ascontiguousarray(np.asarray(r.results[0]["out_t"]).T).reshape(B, S, D)
```

```python
from contextlib import ExitStack

import numpy as np

import concourse.bass as bass
from concourse import mybir

F32 = mybir.dt.float32
F32R = mybir.dt.float32r
I32 = mybir.dt.int32
ALU = mybir.AluOpType
ACT = mybir.ActivationFunctionType
AX = mybir.AxisListType

P = 128
B, S, D = 8, 128, 256
HEADS, HD = 8, 32
INTER = 1024
EPS = 1e-6
ROPE_BASE = 10000.0

T = B * S
KT = D // P
QKV = HEADS * HD + 2 * HD
NR = HEADS + 1
HALF = HD // 2
PAIRS = B // 2
HT = T // 2
HB = B // 2
IT = INTER // P
WIDE = 512
SCALE = float(np.float32(1.0) / np.sqrt(np.float32(HD)))

TWO_PI = 2.0 * np.pi


def _cut(x, bits):
    e = np.floor(np.log2(x)) - (bits - 1)
    return float(np.floor(x / 2.0 ** e) * 2.0 ** e)


PI_1 = _cut(TWO_PI, 9)
PI_2 = _cut(TWO_PI - PI_1, 9)
PI_3 = float(np.float32(TWO_PI - PI_1 - PI_2))
ROUND = 1.5 * 2.0 ** 23
COARSE = 256.0
PI_LOW = float(np.nextafter(np.float32(np.pi), np.float32(0)))

C_COND, C_LN1, C_LN2, C_FREQ = 0, KT * B, KT * B + KT, KT * B + 2 * KT
C_SMALL = C_FREQ + HALF
C_IDENT, C_MASK, C_SEL = 0, P, P + HEADS
C_CONST = C_SEL + 2 * P
CHUNKS = 1 + 3 * (IT // 2)
W_RING = 6
WARM_UPS = (9, 7, 2)
STACK = 3
KD = STACK * HD
QK_RING = 4
TAB_STEPS = 13
POOL_WEIGHTS = (1, 2, 2, 2, 2, 1, 0, 0)
SIN_TABLE = "trig_and_small"
MROWS = 2 * 2 * HEADS


def block_program(nc, smalls, pos, x_t, tw1, tw2, wqkv, weights, consts, out_t):
    with ExitStack() as ctx:
        def sb(name, shape, dt=F32):
            return ctx.enter_context(nc.sbuf_tensor(name, shape, dt))

        def sem(name):
            return ctx.enter_context(nc.semaphore(name))

        small = sb("small", [P, C_SMALL])
        pos_i = sb("pos_i", [P, B], I32)
        const = sb("const", [P, C_CONST])
        x = sb("x", [P, KT, T])
        tw1_s = sb("tw1_s", [P, KT, D])
        tw2_s = sb("tw2_s", [P, KT, D])
        wqkv_s, wqkv_h, wqkv_l = (sb("wqkv_" + n, [P, KT, QKV], d) for n, d in (("s", F32), ("h", F32R), ("l", F32R)))
        w_s = sb("w_s", [P, W_RING, WIDE])
        w_h = sb("w_h", [P, CHUNKS, WIDE], F32R)
        w_l = sb("w_l", [P, CHUNKS, WIDE], F32R)
        ones = sb("ones", [P, P])
        eps = sb("eps", [P, 1])
        sel = sb("sel", [MROWS, 2, P], F32R)
        gain1 = sb("gain1", [P, KT, B])
        gain2 = sb("gain2", [P, KT, B])
        norm = sb("norm", [P, KT, HT])
        norm_h = sb("norm_h", [P, KT, T], F32R)
        norm_l = sb("norm_l", [P, KT, T], F32R)
        square = sb("square", [P, KT, HT])
        angle = sb("angle", [P, B, HALF])
        turns = sb("turns", [P, B, HALF])
        wrap = sb("wrap", [P, 2, B, HALF])
        trig = sb("trig", [P, 3, B, HALF])
        rms_ln = sb("rms_ln", [P, B])
        rstd1 = sb("rstd1", [P, B])
        by_cos = sb("by_cos", [P, NR, HD])
        by_sin = sb("by_sin", [P, NR, HD])
        turned = sb("turned", [P, 2, NR, HD])
        parts = sb("parts", [P, 2, NR, STACK, HD], F32R)
        v = sb("v", [P, B, HD])
        q_t = sb("q_t", [KD, QK_RING, HEADS, S], F32R)
        k_t = sb("k_t", [KD, QK_RING, S], F32R)
        top = sb("top", [P, 2, 2, HEADS])
        top_parts = sb("top_parts", [P, 2, 2, 2, HEADS], F32R)
        top_t = sb("top_t", [MROWS, 2, S])
        top_rows = sb("top_rows", [MROWS, 2, HEADS, S], F32R)
        prob = sb("prob", [P, 2, HEADS, S])
        sum_ln = sb("sum_ln", [P, KT * S])
        sum_inv = sb("sum_inv", [P, 2, KT * S])
        ctx_n = sb("ctx_n", [P, 2, KT, S])
        ctx_h = sb("ctx_h", [P, KT, T], F32R)
        ctx_l = sb("ctx_l", [P, KT, T], F32R)
        rstd2 = sb("rstd2", [P, HT])
        gate = sb("gate", [P, 2, WIDE])
        act = sb("act", [P, 2, WIDE])
        act_h = sb("act_h", [P, 3, WIDE], F32R)
        act_l = sb("act_l", [P, 3, WIDE], F32R)

        def bank(name):
            return ctx.enter_context(nc.psum_tensor(name, [P, WIDE], F32))

        a_ring = [bank(f"a_ring{i}") for i in range(2)]
        v_ring = [bank(f"v_ring{i}") for i in range(2)]
        s_ring = [bank(f"s_ring{i}") for i in range(2)]
        qkv_bank = bank("qkv_bank")
        pv_bank = bank("pv_bank")

        ld_small, ld_pos, ld_tw1, ld_tw2 = sem("ld_small"), sem("ld_pos"), sem("ld_tw1"), sem("ld_tw2")
        ld_x = [sem(f"ld_x{i}") for i in range(PAIRS)]
        ld_wqkv, ld_const = sem("ld_wqkv"), sem("ld_const")
        ld_w = [sem(f"ld_w{i}") for i in range(W_RING)]
        ones_ready, eps_ready, sel_ready = sem("ones_ready"), sem("eps_ready"), sem("sel_ready")
        scale1_done, scale2_done, gain1_ready, gain2_ready = sem("scale1_done"), sem("scale2_done"), sem("gain1_ready"), sem("gain2_ready")
        tab_step = sem("tab_step")
        trig_ready, table_ready = sem("trig_ready"), sem("table_ready")
        sq_ready, ss_done, ln1_ready, rstd1_ready = sem("sq_ready"), sem("ss_done"), sem("ln1_ready"), sem("rstd1_ready")
        xg_ready, xh_ready, xl_ready = sem("xg_ready"), sem("xh_ready"), sem("xl_ready")
        xl_late_ready = sem("xl_late_ready")
        wqkvh_ready, wqkvl_ready = sem("wqkvh_ready"), sem("wqkvl_ready")
        wh_ready, wl_ready = sem("wh_ready"), sem("wl_ready")
        qkv_done, qkv_read = sem("qkv_done"), sem("qkv_read")
        rope_step = sem("rope_step")
        turned_ready, hi_ready, lo_ready = sem("turned_ready"), sem("hi_ready"), sem("lo_ready")
        a_full, a_free = sem("a_full"), sem("a_free")
        v_full, v_free = sem("v_full"), sem("v_free")
        top_hi, top_ready, rows_ready, top_t_ready = sem("top_hi"), sem("top_ready"), sem("rows_ready"), sem("top_t_ready")
        s_full, s_free = sem("s_full"), sem("s_free")
        pv_done, sumln_ready, suminv_ready, ctxn_ready, ctxh_ready, ctxl_ready = (
            sem("pv_done"), sem("sumln_ready"), sem("suminv_ready"), sem("ctxn_ready"), sem("ctxh_ready"), sem("ctxl_ready"))
        wo1_done, x2_ready = sem("wo1_done"), sem("x2_ready")
        sq2_ready, xg2_ready, rstd2_ready = sem("sq2_ready"), sem("xg2_ready"), sem("rstd2_ready")
        h2_ready, h2h_ready, h2l_ready = sem("h2_ready"), sem("h2h_ready"), sem("h2l_ready")
        acth_ready, actl_ready = sem("acth_ready"), sem("actl_ready")
        down_done = sem("down_done")
        y_ready, stored = sem("y_ready"), sem("stored")

        ident = const[:, C_IDENT:C_IDENT + P]

        def toks(b, n=1):
            return slice(b * S, (b + n) * S)

        def half(h):
            return slice(h * HT, (h + 1) * HT)

        def gate_chunk(i):
            return 1 + 3 * (i // 2)

        def qkv_of(b):
            return {1: s_ring[1], 2: s_ring[0]}.get(b, qkv_bank)

        def pv_of(b):
            return qkv_bank if b == B - 1 else pv_bank

        A_ORDER, V_ORDER = [], []
        for s in range(B):
            A_ORDER += [("k", s), ("q", s, 0)]
            if s % 2 == 0 and s >= 2:
                A_ORDER.append(("top", s // 2 - 1))
            A_ORDER.append(("q", s, 1))
            V_ORDER += [("s1", s, 0), ("s1", s, 1)]
        A_ORDER += [("top", PAIRS - 1), ("ss", 0)]
        V_ORDER += [("wo", 0, 0), ("wo", 0, 1)]
        for h in range(2):
            for i in range(IT):
                A_ORDER.append(("g", h, i))
                V_ORDER.append(("u", h, i))
                if h == 0 and i == 4:
                    A_ORDER.append(("ss", 1))
        A_AT = {k: n for n, k in enumerate(A_ORDER)}
        V_AT = {k: n for n, k in enumerate(V_ORDER)}

        block = ctx.enter_context(nc.Block())

        @block.sync
        def _(sp):
            sp.dma_start(small[:, :], smalls).then_inc(ld_small, 16)
            sp.dma_start(tw1_s[:, :, :], tw1.rearrange("(k p) n -> p k n", p=P)).then_inc(ld_tw1, 16)
            xd = x_t.rearrange("(k p) n -> p k n", p=P)
            for p in range(PAIRS):
                sp.dma_start(x[:, :, toks(2 * p, 2)], xd[:, :, toks(2 * p, 2)]).then_inc(ld_x[p], 16)
                if p == 0:
                    sp.dma_start(wqkv_s[:, :, :], wqkv.rearrange("(k p) n -> p k n", p=P)).then_inc(ld_wqkv, 16)
            sp.dma_start(const[:, :], consts).then_inc(ld_const, 16)
            sp.dma_start(tw2_s[:, :, :], tw2.rearrange("(k p) n -> p k n", p=P)).then_inc(ld_tw2, 16)
            for n in range(CHUNKS):
                if n >= W_RING:
                    sp.wait_ge(wl_ready, n - W_RING + 1)
                sp.dma_start(w_s[:, n % W_RING, :], weights[:, n, :]).then_inc(ld_w[n % W_RING], 16)
            od = out_t.rearrange("(k p) n -> p k n", p=P)
            for h in range(2):
                for m in range(KT):
                    sp.wait_ge(y_ready, KT * h + m + 1)
                    sp.dma_start(od[:, m, half(h)], x[:, m, half(h)]).then_inc(stored, 16)
            sp.wait_ge(stored, 16 * 2 * KT)

        @block.tensor
        def _(pe):
            def a_slot(key):
                n = A_AT[key]
                if n >= 2:
                    pe.wait_ge(a_free, n - 1)
                return a_ring[n % 2]

            def v_slot(key):
                n = V_AT[key]
                if n >= 2:
                    pe.wait_ge(v_free, n - 1)
                return v_ring[n % 2]

            def three_pass(dst, pairs, first=True, last=True):
                terms = [t for wh, wl, xh, xl in pairs for t in ((wh, xh), (wh, xl), (wl, xh))]
                for n, (w, d) in enumerate(terms):
                    mm = pe.matmul(dst, w, d, start=first and n == 0, stop=last and n == len(terms) - 1)
                return mm

            def scales(tw, ld, dst, done):
                pe.wait_ge(ld, 16)
                for m in range(KT):
                    for k in range(KT):
                        mm = pe.matmul(dst[:, m * B:(m + 1) * B], tw[:, k, m * P:(m + 1) * P],
                                       small[:, C_COND + k * B:C_COND + (k + 1) * B], start=k == 0, stop=k == KT - 1)
                mm.then_inc(done, 1)

            def project(b):
                pe.wait_ge(xh_ready, b // 2 + 1)
                if b < 2:
                    pe.wait_ge(xl_ready, 1)
                else:
                    pe.wait_ge(xl_late_ready, b // 2)
                if b >= 3:
                    pe.wait_ge(qkv_read, 1 if b == 3 else b)
                dst = qkv_of(b)[:, 0:QKV]
                terms = [t for k in range(KT) for t in (
                    (norm_h[:, k, toks(b)], wqkv_h[:, k, :]), (norm_l[:, k, toks(b)], wqkv_h[:, k, :]),
                    (norm_h[:, k, toks(b)], wqkv_l[:, k, :]))]
                for n, (w, d) in enumerate(terms):
                    mm = pe.matmul(dst, w, d, start=n == 0, stop=n == len(terms) - 1)
                mm.then_inc(qkv_done, 1)

            def turn_key(b):
                pe.wait_ge(hi_ready, 2 * (b + 1))
                pe.wait_ge(lo_ready, 2 * (b + 1))
                dst = a_slot(("k", b))
                pe.transpose(dst[0:KD, 0:S], parts[:, b % 2, HEADS, :, :].rearrange("p a d -> p (a d)").bitcast(F32),
                             ident).then_inc(a_full, 1)

            def turn_queries(b, g):
                dst = a_slot(("q", b, g))
                for j in range(4):
                    mm = pe.transpose(dst[0:KD, j * S:(j + 1) * S],
                                      parts[:, b % 2, 4 * g + j, :, :].rearrange("p a d -> p (a d)").bitcast(F32), ident)
                mm.then_inc(a_full, 1)

            def scores(b, g):
                pe.wait_ge(a_free, A_AT[("q", b, g)] + 1)
                dst = v_slot(("s1", b, g))
                for j in range(4):
                    mm = pe.matmul(dst[:, j * S:(j + 1) * S], q_t[:, b % QK_RING, 4 * g + j, :], k_t[:, b % QK_RING, :],
                                   start=True, stop=True)
                mm.then_inc(v_full, 1)

            def turn_top(p):
                pe.wait_ge(top_ready, p + 1)
                dst = a_slot(("top", p))
                pe.transpose(dst[0:MROWS, 0:S],
                             top_parts[:, p % 2, :, :, :].rearrange("p a b h -> p (a b h)").bitcast(F32),
                             ident).then_inc(a_full, 1)

            def scores_t(b, g):
                pe.wait_ge(rows_ready, b // 2 * 2 + g + 1)
                n = 2 * b + g
                if n >= 2:
                    pe.wait_ge(s_free, n - 1)
                elif n == 0:
                    pe.wait_ge(qkv_read, 3)
                dst = s_ring[n % 2][:, :]
                heads = slice(4 * g, 4 * g + 4)
                pe.matmul(dst, k_t[:, b % QK_RING, :], q_t[:, b % QK_RING, heads, :].rearrange("p h t -> p (h t)"),
                          start=True, stop=False)
                pe.matmul(dst, sel[:, b % 2, :], top_rows[:, b // 2 % 2, heads, :].rearrange("p h t -> p (h t)"),
                          start=False, stop=True).then_inc(s_full, 1)

            def values(b):
                pe.wait_ge(s_free, 2 * b + 2)
                if b == B - 1:
                    pe.wait_ge(qkv_read, B)
                elif b >= 1:
                    pe.wait_ge(ctxn_ready, b)
                for n, w in enumerate((v[:, b, :], ones[:, 0:HD])):
                    for t in range(KT):
                        for j in range(4):
                            at = n * KT * S + t * S
                            mm = pe.matmul(pv_of(b)[HD * j:HD * (j + 1), at:at + S], w, prob[:, b % 2, 4 * t + j, :],
                                           start=True, stop=True, tile_position=(0, HD * j))
                mm.then_inc(pv_done, 1)

            def out_project(h, m):
                pe.wait_ge(wl_ready, 1)
                pe.wait_ge(ctxh_ready, HB * (h + 1))
                pe.wait_ge(ctxl_ready, HB * (h + 1))
                dst = pv_of(B - 2 + m) if h else v_slot(("wo", h, m))
                cols = [slice(k * D + m * P, k * D + (m + 1) * P) for k in range(KT)]
                three_pass(dst[:, :], [(w_h[:, 0, cols[k]], w_l[:, 0, cols[k]], ctx_h[:, k, half(h)], ctx_l[:, k, half(h)])
                                       for k in range(KT)]).then_inc(wo1_done if h else v_full, 1)

            def sum_squares(h):
                dst = a_slot(("ss", h))
                for k in range(KT):
                    pe.wait_ge(sq2_ready, KT * h + k + 1)
                    mm = pe.matmul(dst[:, :], ones[:, :], square[:, k, :], start=k == 0, stop=k == KT - 1)
                mm.then_inc(a_full, 1)

            def gate_up(h, i):
                if i == 0:
                    pe.wait_ge(h2h_ready, KT * (h + 1))
                    pe.wait_ge(h2l_ready, KT * (h + 1))
                pe.wait_ge(wl_ready, gate_chunk(i) + 2)
                for slot, key, n, full in ((a_slot, "g", gate_chunk(i), a_full), (v_slot, "u", gate_chunk(i) + 1, v_full)):
                    dst = slot((key, h, i))
                    cols = [slice(k * 2 * P + i % 2 * P, k * 2 * P + i % 2 * P + P) for k in range(KT)]
                    three_pass(dst[:, :], [(w_h[:, n, cols[k]], w_l[:, n, cols[k]], norm_h[:, k, half(h)], norm_l[:, k, half(h)])
                                           for k in range(KT)]).then_inc(full, 1)

            def down(h, i):
                n = h * IT + i
                chunk = gate_chunk(i) + 2
                pe.wait_ge(wl_ready, chunk + 1)
                pe.wait_ge(actl_ready, n + 1)
                if i == 0 and h == 0:
                    pe.wait_ge(s_free, 2 * B)
                if i == 0 and h == 1:
                    pe.wait_ge(y_ready, KT)
                for m in range(KT):
                    r = slice(i % 2 * D + m * P, i % 2 * D + (m + 1) * P)
                    mm = three_pass(s_ring[m][:, :], [(w_h[:, chunk, r], w_l[:, chunk, r], act_h[:, n % 3, :], act_l[:, n % 3, :])],
                                    first=i == 0, last=i == IT - 1)
                mm.then_inc(down_done, 1)

            def warm_up(n):
                for _ in range(n):
                    pe.matmul(s_ring[0][:, 0:P], ones[:, :], ones[:, :], start=True, stop=True)

            def first_squares(p):
                pe.wait_ge(sq_ready, p + 1)
                for b in range(2):
                    for k in range(KT):
                        mm = pe.matmul(pv_bank[:, 2 * p + b:2 * p + b + 1], square[:, k, toks(2 * (p % 2) + b)], ones[:, 0:1],
                                       start=k == 0, stop=k == KT - 1)
                mm.then_inc(ss_done, 1)

            pe.wait_ge(ones_ready, 1)
            warm_up(WARM_UPS[0])
            pe.wait_ge(ld_small, 16)
            scales(tw1_s, ld_tw1, v_ring[0], scale1_done)
            warm_up(WARM_UPS[1])
            pe.wait_ge(wqkvh_ready, 1)
            pe.wait_ge(wqkvl_ready, 1)
            project(0)
            first_squares(0)
            project(1)
            scales(tw2_s, ld_tw2, v_ring[1], scale2_done)
            first_squares(1)
            warm_up(WARM_UPS[2])
            pe.wait_ge(ld_const, 16)
            for s in range(B):
                turn_key(s)
                turn_queries(s, 0)
                if s == 3:
                    pe.wait_ge(sel_ready, 1)
                if s >= 3:
                    scores_t(s - 3, 0)
                if s % 2 == 0 and s >= 2:
                    turn_top(s // 2 - 1)
                turn_queries(s, 1)
                if s >= 3:
                    scores_t(s - 3, 1)
                if s == 0:
                    project(2)
                    first_squares(2)
                    pe.wait_ge(gain1_ready, KT)
                    pe.wait_ge(gain2_ready, KT)
                if s == 2:
                    first_squares(3)
                scores(s, 0)
                if 1 <= s < B - 2:
                    project(s + 2)
                if s == 3:
                    pe.wait_ge(ln1_ready, PAIRS)
                if s >= 3:
                    values(s - 3)
                scores(s, 1)
            out_project(0, 0)
            turn_top(PAIRS - 1)
            scores_t(B - 3, 0)
            out_project(0, 1)
            scores_t(B - 3, 1)
            scores_t(B - 2, 0)
            sum_squares(0)
            values(B - 3)
            scores_t(B - 2, 1)
            scores_t(B - 1, 0)
            values(B - 2)
            scores_t(B - 1, 1)
            gate_up(0, 0)
            values(B - 1)
            gate_up(0, 1)
            out_project(1, 0)
            out_project(1, 1)
            for h in range(2):
                for i in range(IT):
                    if h == 1 or i >= 2:
                        gate_up(h, i)
                    if i >= 2:
                        down(h, i - 2)
                    if h == 0 and i == 4:
                        sum_squares(1)
                down(h, IT - 2)
                down(h, IT - 1)

        @block.scalar
        def _(act_e):
            act_e.dma_start(pos_i[:, :], pos).then_inc(ld_pos, 16)

            def copy(dst, src):
                return nc.scalar.activation(dst, src, ACT.Copy)

            def cut_x(p):
                act_e.wait_ge(xg_ready, p + 1)
                copy(norm_h[:, :, toks(2 * p, 2)], norm[:, :, toks(2 * (p % 2), 2)]).then_inc(xh_ready, 1)

            def square_x(p):
                act_e.wait_ge(ld_x[p], 16)
                if p >= 2:
                    act_e.wait_ge(ss_done, p - 1)
                nc.scalar.activation(square[:, :, toks(2 * (p % 2), 2)], x[:, :, toks(2 * p, 2)], ACT.Square).then_inc(sq_ready, 1)

            def cut_weight(n):
                act_e.wait_ge(ld_w[n % W_RING], 16 * (n // W_RING + 1))
                copy(w_h[:, n, :], w_s[:, n % W_RING, :]).then_inc(wh_ready, 1)

            def take(key):
                n = A_AT[key]
                act_e.wait_ge(a_full, n + 1)
                return a_ring[n % 2]

            def take_key(b):
                if b >= QK_RING:
                    act_e.wait_ge(s_full, 2 * (b - QK_RING) + 2)
                src = take(("k", b))
                copy(k_t[:, b % QK_RING, :], src[0:KD, 0:S]).then_inc(a_free, 1)

            def take_queries(b, g):
                src = take(("q", b, g))
                copy(q_t[:, b % QK_RING, 4 * g:4 * g + 4, :],
                     src[0:KD, :].rearrange("p (h t) -> p h t", h=4)).then_inc(a_free, 1)

            def take_top(p):
                src = take(("top", p))
                if p >= 2:
                    act_e.wait_ge(rows_ready, 2 * (p - 1))
                nc.scalar.activation(top_t[:, p % 2, :], src[0:MROWS, 0:S], ACT.Copy).then_inc(a_free, 1)

            def exps(b, g):
                if b >= 2 and g == 0:
                    act_e.wait_ge(pv_done, b - 1)
                n = 2 * b + g
                act_e.wait_ge(s_full, n + 1)
                nc.scalar.activation(prob[:, b % 2, 4 * g:4 * g + 4, :], s_ring[n % 2][:, :].rearrange("p (h t) -> p h t", h=4),
                                     ACT.Exp, scale=SCALE).then_inc(s_free, 1)

            def invert_sums(b):
                act_e.wait_ge(pv_done, b + 1)
                if b >= 1:
                    act_e.wait_ge(suminv_ready, b)
                nc.scalar.activation(sum_ln[:, :], pv_of(b)[:, KT * S:2 * KT * S], ACT.Ln).then_inc(sumln_ready, 1)
                act_e.wait_ge(sumln_ready, b + 1)
                if b >= 2:
                    act_e.wait_ge(ctxn_ready, b - 1)
                nc.scalar.activation(sum_inv[:, b % 2, :], sum_ln[:, :], ACT.Exp, scale=-1.0).then_inc(suminv_ready, 1)

            def cut_ctx(b):
                act_e.wait_ge(ctxn_ready, b + 1)
                copy(ctx_h[:, :, toks(b)], ctx_n[:, b % 2, :, :]).then_inc(ctxh_ready, 1)

            def square_x2(h, m):
                if h:
                    act_e.wait_ge(a_full, A_AT[("ss", 0)] + 1)
                    act_e.wait_ge(x2_ready, m + 1)
                else:
                    act_e.wait_ge(ss_done, PAIRS)
                    act_e.wait_ge(v_free, V_AT[("wo", 0, m)] + 1)
                nc.scalar.activation(square[:, m, :], x[:, m, half(h)], ACT.Square).then_inc(sq2_ready, 1)

            def root2(h):
                src = take(("ss", h))
                if h:
                    act_e.wait_ge(h2_ready, KT * h)
                nc.scalar.activation(rstd2[:, :], src[:, :], ACT.Ln, scale=1.0 / D, bias=eps[:, 0:1]).then_inc(a_free, 1)
                act_e.wait_ge(a_free, A_AT[("ss", h)] + 1)
                nc.scalar.activation(rstd2[:, :], rstd2[:, :], ACT.Exp, scale=-0.5).then_inc(rstd2_ready, 1)

            def cut_h2(h):
                for k in range(KT):
                    act_e.wait_ge(h2_ready, KT * h + k + 1)
                    copy(norm_h[:, k, half(h)], norm[:, k, :]).then_inc(h2h_ready, 1)

            def silu(h, i):
                n = h * IT + i
                src = take(("g", h, i))
                if n >= 2:
                    act_e.wait_ge(v_free, V_AT[("u",) + divmod(n - 2, IT)] + 1)
                nc.scalar.activation(gate[:, n % 2, :], src[:, :], ACT.Silu).then_inc(a_free, 1)

            def root1(p):
                act_e.wait_ge(ss_done, p + 1)
                r = slice(2 * p, 2 * p + 2)
                nc.scalar.activation(rms_ln[:, r], pv_bank[:, r], ACT.Ln, scale=1.0 / D, bias=eps[:, 0:1]).then_inc(ln1_ready, 1)
                act_e.wait_ge(ln1_ready, p + 1)
                nc.scalar.activation(rstd1[:, r], rms_ln[:, r], ACT.Exp, scale=-0.5).then_inc(rstd1_ready, 1)

            def cut_weights(n):
                for i in range(n):
                    if chunk[0] < CHUNKS:
                        cut_weight(chunk[0])
                        chunk[0] += 1

            act_e.wait_ge(eps_ready, 1)
            nc.scalar.preload_act_table_set(SIN_TABLE)
            square_x(0)
            act_e.wait_ge(ld_wqkv, 16)
            copy(wqkv_h[:, :, :], wqkv_s[:, :, :]).then_inc(wqkvh_ready, 1)
            cut_x(0)
            act_e.wait_ge(tab_step, TAB_STEPS)
            nc.scalar.activation(trig[:, 0:2, :, :], wrap[:, :, :, :], ACT.Sin).then_inc(trig_ready, 1)
            nc.scalar.activation(trig[:, 2, :, :], wrap[:, 0, :, :], ACT.Sin, scale=-1.0).then_inc(trig_ready, 1)
            nc.scalar.preload_act_table_set("natural_log_exp_and_others")
            root1(0)
            square_x(1)
            cut_x(1)
            root1(1)
            square_x(2)
            chunk = [0]
            cut_weights(1)
            for s in range(B):
                if s >= 4:
                    invert_sums(s - 4)
                take_key(s)
                take_queries(s, 0)
                if s % 2 == 0 and s >= 2:
                    take_top(s // 2 - 1)
                if s >= 3:
                    exps(s - 3, 0)
                take_queries(s, 1)
                if s >= 3:
                    exps(s - 3, 1)
                if s >= 4:
                    cut_ctx(s - 4)
                if s == 0:
                    root1(2)
                    cut_x(2)
                if s == 1:
                    square_x(3)
                    cut_x(3)
                    act_e.wait_ge(ld_const, 16)
                    copy(sel[:, :, :], const[0:MROWS, C_SEL:C_SEL + 2 * P].rearrange("p (b n) -> p b n", b=2)).then_inc(sel_ready, 1)
                if s == 2:
                    root1(3)
                cut_weights(2 if s else 1)
            take_top(PAIRS - 1)
            invert_sums(B - 4)
            exps(B - 3, 0)
            square_x2(0, 0)
            exps(B - 3, 1)
            square_x2(0, 1)
            exps(B - 2, 0)
            cut_ctx(B - 4)
            root2(0)
            invert_sums(B - 3)
            exps(B - 2, 1)
            cut_h2(0)
            exps(B - 1, 0)
            cut_ctx(B - 3)
            invert_sums(B - 2)
            exps(B - 1, 1)
            cut_ctx(B - 2)
            invert_sums(B - 1)
            cut_ctx(B - 1)
            assert chunk[0] == CHUNKS
            for h in range(2):
                for i in range(IT):
                    silu(h, i)
                    if h == 0 and i == 2:
                        square_x2(1, 0)
                        square_x2(1, 1)
                    if h == 0 and i == 4:
                        root2(1)
                        cut_h2(1)

        @block.vector
        def _(dve):
            ve = nc.vector
            table = [0]

            def tab(ins):
                table[0] += 1
                ins.then_inc(tab_step, 1)
                dve.wait_ge(tab_step, table[0])

            def count_turns(count_scale):
                tab(ve.tensor_scalar(turns[:, :, :], angle[:, :, :], count_scale, ROUND, ALU.mult, ALU.add))
                tab(ve.tensor_scalar(turns[:, :, :], turns[:, :, :], -ROUND, None, ALU.add))

            def take_turns(unit):
                for part in (PI_1, PI_2, PI_3):
                    tab(ve.scalar_tensor_tensor(out=angle[:, :, :], in0=turns[:, :, :], scalar=-part * unit,
                                                in1=angle[:, :, :], op0=ALU.mult, op1=ALU.add))

            def gain(scale, c_ln, dst, done, ready):
                dve.wait_ge(done, 1)
                for k in range(KT):
                    ve.tensor_scalar(dst[:, k, :], scale[:, k * B:(k + 1) * B], 1.0, small[:, c_ln + k:c_ln + k + 1],
                                     ALU.add, ALU.mult).then_inc(ready, 1)

            def gain_x(p):
                r = toks(2 * p, 2)
                dve.wait_ge(ld_x[p], 16)
                dve.wait_ge(gain1_ready, KT)
                if p >= 2:
                    dve.wait_ge(xh_ready, p - 1)
                    (dve.wait_ge(xl_ready, 1) if p == 2 else dve.wait_ge(xl_late_ready, 1))
                ve.tensor_tensor(norm[:, :, toks(2 * (p % 2), 2)].rearrange("p k (b t) -> p k b t", b=2),
                                 x[:, :, r].rearrange("p k (b t) -> p k b t", b=2),
                                 gain1[:, :, 2 * p:2 * p + 2].unsqueeze(3).to_broadcast([P, KT, 2, S]),
                                 ALU.mult).then_inc(xg_ready, 1)

            def rest_x(p):
                r = toks(2 * p, 2)
                dve.wait_ge(xh_ready, p + 1)
                ve.tensor_tensor(norm_l[:, :, r], norm[:, :, toks(2 * (p % 2), 2)], norm_h[:, :, r].bitcast(F32), ALU.subtract).then_inc(xl_ready, 1)

            def rotate(b):
                s = b % 2
                dve.wait_ge(qkv_done, b + 1)
                if b >= 2:
                    dve.wait_ge(a_full, A_AT[("q", b - 2, 1)] + 1)
                bank_b = qkv_of(b)
                src = bank_b[:, 0:NR * HD].rearrange("p (h a d) -> p h a d", h=NR, a=2)
                if b == 0:
                    dve.wait_ge(trig_ready, 2)
                ve.tensor_tensor(by_cos[:, :, :].rearrange("p h (a d) -> p h a d", a=2), src,
                                 trig[:, 1, b, :].unsqueeze(1).unsqueeze(1).to_broadcast([P, NR, 2, HALF]),
                                 ALU.mult).then_inc(rope_step, 1)
                dve.wait_ge(rstd1_ready, b // 2 + 1)
                for a, sine in ((0, 2), (1, 0)):
                    ve.scalar_tensor_tensor(out=by_sin[:, :, :].rearrange("p h (a d) -> p h a d", a=2)[:, :, a, :], in0=src[:, :, 1 - a, :],
                                            scalar=rstd1[:, b:b + 1], in1=trig[:, sine, b, :].unsqueeze(1).to_broadcast([P, NR, HALF]),
                                            op0=ALU.mult, op1=ALU.mult).then_inc(rope_step, 1)
                ve.tensor_scalar(v[:, b, :], bank_b[:, NR * HD:QKV], rstd1[:, b:b + 1], None, ALU.mult).then_inc(qkv_read, 1)
                dve.wait_ge(rope_step, 3 * (b + 1))
                ve.scalar_tensor_tensor(out=turned[:, s, :, :], in0=by_cos[:, :, :], scalar=rstd1[:, b:b + 1], in1=by_sin[:, :, :],
                                        op0=ALU.mult, op1=ALU.add).then_inc(turned_ready, 1)
                dve.wait_ge(turned_ready, b + 1)
                ve.tensor_copy(parts[:, s, HEADS, 0:2, :],
                               turned[:, s, HEADS, :].unsqueeze(1).to_broadcast([P, 2, HD])).then_inc(hi_ready, 1)
                ve.tensor_copy(parts[:, s, 0:HEADS, 0:STACK:2, :],
                               turned[:, s, 0:HEADS, :].unsqueeze(2).to_broadcast([P, HEADS, 2, HD])).then_inc(hi_ready, 1)
                for n, (heads, lo) in enumerate(((slice(HEADS, NR), 2), (slice(0, HEADS), 1))):
                    dve.wait_ge(hi_ready, 2 * b + n + 1)
                    ve.tensor_tensor(parts[:, s, heads, lo, :], turned[:, s, heads, :],
                                     parts[:, s, heads, 0, :].bitcast(F32), ALU.subtract).then_inc(lo_ready, 1)

            def maxima(b, g):
                n = V_AT[("s1", b, g)]
                dve.wait_ge(v_full, n + 1)
                if g == 0 and b >= 4:
                    dve.wait_ge(top_ready, b // 2 - 1)
                ve.tensor_reduce(top[:, b // 2 % 2, b % 2, 4 * g:4 * g + 4],
                                 v_ring[n % 2][:, :].rearrange("p (h k) -> p h k", h=4), AX.X, ALU.max).then_inc(v_free, 1)

            def cut_top(p):
                dve.wait_ge(v_free, V_AT[("s1", 2 * p + 1, 1)] + 1)
                if p >= 2:
                    dve.wait_ge(a_full, A_AT[("top", p - 2)] + 1)
                ve.tensor_copy(top_parts[:, p % 2, 0, :, :], top[:, p % 2, :, :]).then_inc(top_hi, 1)
                dve.wait_ge(top_hi, p + 1)
                ve.tensor_tensor(top_parts[:, p % 2, 1, :, :], top[:, p % 2, :, :],
                                 top_parts[:, p % 2, 0, :, :].bitcast(F32), ALU.subtract).then_inc(top_ready, 1)

            def norm_ctx(b):
                dve.wait_ge(suminv_ready, b + 1)
                if b >= 2:
                    dve.wait_ge(ctxh_ready, b - 1)
                    dve.wait_ge(ctxl_ready, b - 1)
                ve.tensor_tensor(ctx_n[:, b % 2, :, :].rearrange("p k t -> p (k t)"), pv_of(b)[:, 0:KT * S],
                                 sum_inv[:, b % 2, :], ALU.mult).then_inc(ctxn_ready, 1)

            def residual1(h, m):
                if h:
                    dve.wait_ge(wo1_done, m + 1)
                    src, done = pv_of(B - 2 + m), x2_ready
                else:
                    n = V_AT[("wo", 0, m)]
                    dve.wait_ge(v_full, n + 1)
                    src, done = v_ring[n % 2], v_free
                ve.tensor_tensor(x[:, m, half(h)], src[:, :], x[:, m, half(h)], ALU.add).then_inc(done, 1)

            def scale_h2(h):
                dve.wait_ge(rstd2_ready, h + 1)
                for k in range(KT):
                    dve.wait_ge(xg2_ready, KT * h + k + 1)
                    ve.tensor_tensor(norm[:, k, :], norm[:, k, :], rstd2[:, :], ALU.mult).then_inc(h2_ready, 1)

            def rest_h2(h):
                for k in range(KT):
                    dve.wait_ge(h2h_ready, KT * h + k + 1)
                    ve.tensor_tensor(norm_l[:, k, half(h)], norm[:, k, :], norm_h[:, k, half(h)].bitcast(F32),
                                     ALU.subtract).then_inc(h2l_ready, 1)

            def activate(h, i):
                n = h * IT + i
                at = V_AT[("u", h, i)]
                dve.wait_ge(v_full, at + 1)
                dve.wait_ge(a_free, A_AT[("g", h, i)] + 1)
                if n >= 3:
                    dve.wait_ge(down_done, n - 2)
                ve.tensor_tensor(act[:, n % 2, :], v_ring[at % 2][:, :], gate[:, n % 2, :], ALU.mult).then_inc(v_free, 1)
                dve.wait_ge(v_free, at + 1)
                ve.tensor_copy(act_h[:, n % 3, :], act[:, n % 2, :]).then_inc(acth_ready, 1)
                dve.wait_ge(acth_ready, n + 1)
                ve.tensor_tensor(act_l[:, n % 3, :], act[:, n % 2, :], act_h[:, n % 3, :].bitcast(F32),
                                 ALU.subtract).then_inc(actl_ready, 1)

            def residual2(h):
                dve.wait_ge(down_done, IT * (h + 1))
                for m in range(KT):
                    ve.tensor_tensor(x[:, m, half(h)], s_ring[m][:, :], x[:, m, half(h)], ALU.add).then_inc(y_ready, 1)

            ve.memset(eps[:, :], EPS).then_inc(eps_ready, 1)
            dve.wait_ge(ld_pos, 16)
            dve.wait_ge(ld_small, 16)
            tab(ve.tensor_tensor(angle[:, :, :], pos_i[:, :].unsqueeze(2).to_broadcast([P, B, HALF]),
                                 small[:, C_FREQ:C_FREQ + HALF].unsqueeze(1).to_broadcast([P, B, HALF]), ALU.mult))
            count_turns(1.0 / (TWO_PI * COARSE))
            take_turns(COARSE)
            count_turns(1.0 / TWO_PI)
            take_turns(1.0)
            gain(v_ring[0], C_LN1, gain1, scale1_done, gain1_ready)
            gain_x(0)
            ve.tensor_scalar(turns[:, :, :], angle[:, :, :], float(np.pi / 2), -TWO_PI, ALU.is_gt, ALU.mult).then_inc(table_ready, 1)
            tab(ve.tensor_scalar(wrap[:, 0, :, :], angle[:, :, :], PI_LOW, -PI_LOW, ALU.min, ALU.max))
            dve.wait_ge(table_ready, 1)
            ve.scalar_tensor_tensor(out=angle[:, :, :], in0=angle[:, :, :], scalar=float(np.pi / 2), in1=turns[:, :, :],
                                    op0=ALU.add, op1=ALU.add).then_inc(table_ready, 1)
            dve.wait_ge(table_ready, 2)
            tab(ve.tensor_scalar(wrap[:, 1, :, :], angle[:, :, :], PI_LOW, -PI_LOW, ALU.min, ALU.max))
            assert table[0] == TAB_STEPS
            rest_x(0)
            gain_x(1)
            rotate(0)
            gain(v_ring[1], C_LN2, gain2, scale2_done, gain2_ready)
            gain_x(2)
            for s in range(B):
                if s >= 4:
                    norm_ctx(s - 4)
                if s + 1 < B:
                    rotate(s + 1)
                maxima(s, 0)
                maxima(s, 1)
                if s == 0:
                    gain_x(3)
                if s % 2:
                    cut_top(s // 2)
            norm_ctx(B - 4)
            residual1(0, 0)
            residual1(0, 1)
            scale_h2(0)
            norm_ctx(B - 3)
            rest_h2(0)
            norm_ctx(B - 2)
            norm_ctx(B - 1)
            for h in range(2):
                for i in range(IT):
                    activate(h, i)
                    if h == 0 and i == 1:
                        residual1(1, 0)
                        residual1(1, 1)
                    if h == 0 and i == 4:
                        scale_h2(1)
                        rest_h2(1)
                residual2(h)

        @block.gpsimd
        def _(pool):
            gp = nc.gpsimd
            gp.memset(ones[:, :], 1.0).then_inc(ones_ready, 1)

            def rest_weight(n):
                pool.wait_ge(wh_ready, n + 1)
                gp.tensor_tensor(w_l[:, n, :], w_s[:, n % W_RING, :], w_h[:, n, :].bitcast(F32), ALU.subtract).then_inc(wl_ready, 1)

            def rest_x(p):
                r = toks(2 * p, 2)
                pool.wait_ge(xh_ready, p + 1)
                gp.tensor_tensor(norm_l[:, :, r], norm[:, :, toks(2 * (p % 2), 2)], norm_h[:, :, r].bitcast(F32), ALU.subtract).then_inc(xl_late_ready, 1)

            def spread_top(p):
                pool.wait_ge(a_free, A_AT[("top", p)] + 1)
                if p >= 2:
                    pool.wait_ge(s_full, 4 * (p - 1))
                for g in range(2):
                    heads = slice(4 * g, 4 * g + 4)
                    gp.tensor_tensor(top_rows[:, p % 2, heads, :], top_t[:, p % 2, :].unsqueeze(1).to_broadcast([MROWS, 4, S]),
                                     const[0:MROWS, C_MASK + 4 * g:C_MASK + 4 * g + 4].unsqueeze(2).to_broadcast([MROWS, 4, S]),
                                     ALU.mult).then_inc(rows_ready, 1)

            def rest_ctx(b):
                pool.wait_ge(ctxh_ready, b + 1)
                gp.tensor_tensor(ctx_l[:, :, toks(b)], ctx_n[:, b % 2, :, :], ctx_h[:, :, toks(b)].bitcast(F32),
                                 ALU.subtract).then_inc(ctxl_ready, 1)

            def gain_x2(h):
                if h:
                    pool.wait_ge(h2l_ready, KT)
                for k in range(KT):
                    if h:
                        pool.wait_ge(x2_ready, k + 1)
                    else:
                        pool.wait_ge(v_free, V_AT[("wo", 0, k)] + 1)
                    gp.tensor_tensor(norm[:, k, :].rearrange("p (b t) -> p b t", b=HB), x[:, k, half(h)].rearrange("p (b t) -> p b t", b=HB),
                                     gain2[:, k, HB * h:HB * (h + 1)].unsqueeze(2).to_broadcast([P, HB, S]),
                                     ALU.mult).then_inc(xg2_ready, 1)

            pool.wait_ge(wqkvh_ready, 1)
            gp.tensor_tensor(wqkv_l[:, :, :], wqkv_s[:, :, :], wqkv_h[:, :, :].bitcast(F32), ALU.subtract).then_inc(wqkvl_ready, 1)
            rest_x(1)
            rest_weight(0)
            chunk = 1
            for s in range(B):
                if s < 2:
                    rest_x(s + 2)
                if s == 2:
                    pool.wait_ge(ld_const, 16)
                if s % 2 == 0 and s >= 2:
                    spread_top(s // 2 - 1)
                if s >= 4:
                    rest_ctx(s - 4)
                for _ in range(POOL_WEIGHTS[s]):
                    rest_weight(chunk)
                    chunk += 1
            spread_top(PAIRS - 1)
            pool.wait_ge(gain2_ready, KT)
            gain_x2(0)
            for b in range(B - 4, B):
                rest_ctx(b)
            for n in range(chunk, CHUNKS):
                rest_weight(n)
            gain_x2(1)


def kernel(x, pos_BxS, cond_2048, L0_cond_ln1_w, L0_cond_ln1_tw, L0_cond_ln2_w, L0_cond_ln2_tw,
           L0_cond_Wq, L0_cond_Wk, L0_cond_Wv, L0_cond_Wo, L0_cond_Wg, L0_cond_Wu, L0_cond_Wd):
    import concourse.bacc as _bacc
    from concourse import mybir as _mybir
    from concourse.bass_utils import run_bass_kernel_spmd as _run

    def rows(a):
        a = np.asarray(a)
        return a.reshape(KT, P, -1).transpose(1, 0, 2).reshape(P, -1)

    def turned(a):
        return np.ascontiguousarray(np.asarray(a).T)

    freq = (np.float32(1.0) / np.float32(ROPE_BASE) ** (np.arange(0, HD, 2, dtype=np.float32) / np.float32(HD))).astype(np.float32)
    const = np.zeros((P, C_CONST), np.float32)
    const[:, C_IDENT:C_IDENT + P] = np.eye(P, dtype=np.float32)
    for r in range(MROWS):
        const[r, C_MASK + r % HEADS] = -1.0
        b = r // HEADS % 2
        const[r, C_SEL + b * P:C_SEL + (b + 1) * P] = 1.0

    w_gate, w_up, w_down = rows(turned(L0_cond_Wg)), rows(turned(L0_cond_Wu)), np.asarray(L0_cond_Wd).T
    chunks = [rows(turned(L0_cond_Wo))]
    for c in range(IT // 2):
        for w in (w_gate, w_up):
            chunks.append(w.reshape(P, KT, INTER)[:, :, 2 * P * c:2 * P * (c + 1)].reshape(P, WIDE))
        chunks.append(w_down[2 * P * c:2 * P * (c + 1)].reshape(2, P, D).transpose(1, 0, 2).reshape(P, WIDE))
    arrays = {
        "smalls": np.concatenate([rows(turned(cond_2048)), rows(np.asarray(L0_cond_ln1_w)[:, None]),
                                  rows(np.asarray(L0_cond_ln2_w)[:, None]), np.broadcast_to(freq, (P, HALF))], axis=1),
        "pos": turned(pos_BxS),
        "x_t": turned(np.asarray(x).reshape(T, D)),
        "tw1": turned(L0_cond_ln1_tw),
        "tw2": turned(L0_cond_ln2_tw),
        "wqkv": np.concatenate([turned(L0_cond_Wq), turned(L0_cond_Wk), turned(L0_cond_Wv)], axis=1),
        "weights": np.stack(chunks, axis=1),
        "consts": const,
    }
    nc = _bacc.Bacc("TRN2", target_bir_lowering=False, num_devices=1)
    feeds, args = {}, []
    for name, a in arrays.items():
        a = np.ascontiguousarray(a)
        feeds[f"in_{name}"] = a
        args.append(nc.dram_tensor(f"in_{name}", a.shape, _mybir.dt.from_np(a.dtype), kind="ExternalInput").ap())
    out = nc.dram_tensor("out_t", (D, T), _mybir.dt.float32, kind="ExternalOutput").ap()
    block_program(nc, *args, out)
    r = _run(nc, [feeds], core_ids=[0])
    return np.ascontiguousarray(np.asarray(r.results[0]["out_t"]).T).reshape(B, S, D)
```

```python
from contextlib import ExitStack

import numpy as np

import concourse.bass as bass
from concourse import mybir

F32 = mybir.dt.float32
F32R = mybir.dt.float32r
I32 = mybir.dt.int32
ALU = mybir.AluOpType
ACT = mybir.ActivationFunctionType
AX = mybir.AxisListType

P = 128
B, S, D = 8, 128, 256
HEADS, HD = 8, 32
INTER = 1024
EPS = 1e-6
ROPE_BASE = 10000.0

T = B * S
KT = D // P
QKV = HEADS * HD + 2 * HD
NR = HEADS + 1
HALF = HD // 2
PAIRS = B // 2
HT = T // 2
HB = B // 2
IT = INTER // P
WIDE = 512
SCALE = float(np.float32(1.0) / np.sqrt(np.float32(HD)))

TWO_PI = 2.0 * np.pi


def _cut(x, bits):
    e = np.floor(np.log2(x)) - (bits - 1)
    return float(np.floor(x / 2.0 ** e) * 2.0 ** e)


PI_1 = _cut(TWO_PI, 9)
PI_2 = _cut(TWO_PI - PI_1, 9)
PI_3 = float(np.float32(TWO_PI - PI_1 - PI_2))
ROUND = 1.5 * 2.0 ** 23
COARSE = 256.0
PI_LOW = float(np.nextafter(np.float32(np.pi), np.float32(0)))

C_COND, C_LN1, C_LN2, C_FREQ = 0, KT * B, KT * B + KT, KT * B + 2 * KT
C_SMALL = C_FREQ + HALF
C_IDENT, C_MASK, C_SEL = 0, P, P + HEADS
C_CONST = C_SEL + 2 * P
CHUNKS = 1 + 3 * (IT // 2)
W_RING = 6
WARM_UPS = (9, 7, 2)
STACK = 3
KD = STACK * HD
QK_RING = 4
TAB_STEPS = 13
ACT_WEIGHTS = (0, 1, 1, 1, 1, 1, 0, 2)
DVE_LO = (0, 3)
POOL_WEIGHTS = (0, 1, 1, 1, 0, 0, 0, 0)
SIN_TABLE = "trig_and_small"
MROWS = 2 * 2 * HEADS
assert KD + MROWS == P


def block_program(nc, smalls, pos, x_t, tw1, tw2, wqkv, weights, consts, out_t):
    with ExitStack() as ctx:
        def sb(name, shape, dt=F32):
            return ctx.enter_context(nc.sbuf_tensor(name, shape, dt))

        def sem(name):
            return ctx.enter_context(nc.semaphore(name))

        small = sb("small", [P, C_SMALL])
        pos_i = sb("pos_i", [P, B], I32)
        const = sb("const", [P, C_CONST])
        x = sb("x", [P, KT, T])
        tw1_s = sb("tw1_s", [P, KT, D])
        tw2_s = sb("tw2_s", [P, KT, D])
        wqkv_s, wqkv_h, wqkv_l = (sb("wqkv_" + n, [P, KT, QKV], d) for n, d in (("s", F32), ("h", F32R), ("l", F32R)))
        w_s = sb("w_s", [P, W_RING, WIDE])
        w_h = sb("w_h", [P, CHUNKS, WIDE], F32R)
        w_l = sb("w_l", [P, CHUNKS, WIDE], F32R)
        ones = sb("ones", [P, P])
        eps = sb("eps", [P, 1])
        gain1 = sb("gain1", [P, KT, B])
        gain2 = sb("gain2", [P, KT, B])
        norm = sb("norm", [P, KT, HT])
        norm_h = sb("norm_h", [P, KT, T], F32R)
        norm_l = sb("norm_l", [P, KT, T], F32R)
        square = sb("square", [P, KT, HT])
        square_h, square_l = sb("square_h", [P, HT], F32R), sb("square_l", [P, HT], F32R)
        ones_r = sb("ones_r", [P, P], F32R)
        angle = sb("angle", [P, B, HALF])
        turns = sb("turns", [P, B, HALF])
        wrap = sb("wrap", [P, 2, B, HALF])
        trig = sb("trig", [P, 3, B, HALF])
        rms_ln = sb("rms_ln", [P, B])
        rstd1 = sb("rstd1", [P, B])
        by_cos = sb("by_cos", [P, NR, HD])
        by_sin = sb("by_sin", [P, NR, HD])
        turned = sb("turned", [P, 2, NR, HD])
        parts = sb("parts", [P, 2, NR, STACK, HD], F32R)
        v = sb("v", [P, B, HD])
        q_t = sb("q_t", [P, QK_RING, HEADS, S], F32R)
        k_t = sb("k_t", [P, QK_RING, S], F32R)
        top = sb("top", [P, 2, 2, HEADS])
        top_parts = sb("top_parts", [P, 2, 2, 2, HEADS], F32R)
        top_t = sb("top_t", [P, 2, S])
        prob = sb("prob", [P, 2, HEADS, S])
        sum_ln = sb("sum_ln", [P, KT * S])
        sum_inv = sb("sum_inv", [P, 2, KT * S])
        ctx_n = sb("ctx_n", [P, 2, KT, S])
        ctx_h = sb("ctx_h", [P, KT, T], F32R)
        ctx_l = sb("ctx_l", [P, KT, T], F32R)
        rstd2 = sb("rstd2", [P, HT])
        gate = sb("gate", [P, 2, WIDE])
        act = sb("act", [P, 2, WIDE])
        act_h = sb("act_h", [P, 3, WIDE], F32R)
        act_l = sb("act_l", [P, 3, WIDE], F32R)

        def bank(name):
            return ctx.enter_context(nc.psum_tensor(name, [P, WIDE], F32))

        a_ring = [bank(f"a_ring{i}") for i in range(2)]
        v_ring = [bank(f"v_ring{i}") for i in range(2)]
        s_ring = [bank(f"s_ring{i}") for i in range(2)]
        qkv_bank = bank("qkv_bank")
        pv_bank = bank("pv_bank")

        ld_small, ld_pos, ld_tw1, ld_tw2 = sem("ld_small"), sem("ld_pos"), sem("ld_tw1"), sem("ld_tw2")
        ld_x = [sem(f"ld_x{i}") for i in range(PAIRS)]
        ld_wqkv, ld_const = sem("ld_wqkv"), sem("ld_const")
        ld_w = [sem(f"ld_w{i}") for i in range(W_RING)]
        ones_ready, eps_ready, sel_ready = sem("ones_ready"), sem("eps_ready"), sem("sel_ready")
        onesr_ready = sem("onesr_ready")
        scale1_done, scale2_done, gain1_ready, gain2_ready = sem("scale1_done"), sem("scale2_done"), sem("gain1_ready"), sem("gain2_ready")
        tab_step = sem("tab_step")
        trig_ready, table_ready = sem("trig_ready"), sem("table_ready")
        sq_ready, ss_done, ln1_ready, rstd1_ready = sem("sq_ready"), sem("ss_done"), sem("ln1_ready"), sem("rstd1_ready")
        xg_ready, xh_ready, xl_ready = sem("xg_ready"), sem("xh_ready"), sem("xl_ready")
        xg_late_ready, xl_late_ready = sem("xg_late_ready"), sem("xl_late_ready")
        wqkvh_ready, wqkvl_ready = sem("wqkvh_ready"), sem("wqkvl_ready")
        wh_ready, wl_ready = sem("wh_ready"), sem("wl_ready")
        qkv_done, qkv_read = sem("qkv_done"), sem("qkv_read")
        rope_step = sem("rope_step")
        turned_ready, hi_ready, lo_ready = sem("turned_ready"), sem("hi_ready"), sem("lo_ready")
        dve_lo_ready = sem("dve_lo_ready")
        a_full, a_free = sem("a_full"), sem("a_free")
        v_full, v_free = sem("v_full"), sem("v_free")
        top_hi, top_ready, rows_ready, top_t_ready = sem("top_hi"), sem("top_ready"), sem("rows_ready"), sem("top_t_ready")
        s_full, s_free = sem("s_full"), sem("s_free")
        pv_done, sumln_ready, suminv_ready, ctxn_ready, ctxh_ready, ctxl_ready = (
            sem("pv_done"), sem("sumln_ready"), sem("suminv_ready"), sem("ctxn_ready"), sem("ctxh_ready"), sem("ctxl_ready"))
        wo1_done, x2_ready = sem("wo1_done"), sem("x2_ready")
        ctxl_last_ready = sem("ctxl_last_ready")
        sq2_ready, xg2_ready, rstd2_ready = sem("sq2_ready"), sem("xg2_ready"), sem("rstd2_ready")
        sq2sum_ready, sq2h_ready, sq2l_ready = sem("sq2sum_ready"), sem("sq2h_ready"), sem("sq2l_ready")
        h2_ready, h2h_ready, h2l_ready = sem("h2_ready"), sem("h2h_ready"), sem("h2l_ready")
        acth_ready, actl_ready = sem("acth_ready"), sem("actl_ready")
        down_done = sem("down_done")
        down0_done = sem("down0_done")
        y_ready, stored = sem("y_ready"), sem("stored")

        ident = const[:, C_IDENT:C_IDENT + P]

        def toks(b, n=1):
            return slice(b * S, (b + n) * S)

        def half(h):
            return slice(h * HT, (h + 1) * HT)

        def gate_chunk(i):
            return 1 + 3 * (i // 2)

        def los_of(b):
            return 2 * sum(j not in DVE_LO for j in range(b + 1))

        def qkv_of(b):
            return {1: s_ring[1], 2: s_ring[0]}.get(b, qkv_bank)

        def pv_of(b):
            return qkv_bank if b >= B - 3 and b % 2 else pv_bank

        A_ORDER, V_ORDER = [], []
        for s in range(B):
            A_ORDER += [("k", s), ("q", s, 0), ("q", s, 1)]
            if s % 2 == 0 and s >= 2:
                A_ORDER.append(("top", s // 2 - 1))
            V_ORDER += [("s1", s, 0), ("s1", s, 1)]
        A_ORDER += [("top", PAIRS - 1), ("ss", 0)]
        V_ORDER += [("wo", 0, 0), ("wo", 0, 1)]
        for h in range(2):
            for i in range(IT):
                A_ORDER.append(("g", h, i))
                V_ORDER.append(("u", h, i))
                if h == 0 and i == 4:
                    A_ORDER.append(("ss", 1))
        A_AT = {k: n for n, k in enumerate(A_ORDER)}
        V_AT = {k: n for n, k in enumerate(V_ORDER)}

        y_parts = [(0, half(0)), (1, half(0)), (0, half(1)), (1, toks(HB, 2)), (1, toks(HB + 2, 2))]

        block = ctx.enter_context(nc.Block())

        @block.sync
        def _(sp):
            sp.dma_start(small[:, :], smalls).then_inc(ld_small, 16)
            sp.dma_start(tw1_s[:, :, :], tw1.rearrange("(k p) n -> p k n", p=P)).then_inc(ld_tw1, 16)
            xd = x_t.rearrange("(k p) n -> p k n", p=P)
            for p in range(PAIRS):
                sp.dma_start(x[:, :, toks(2 * p, 2)], xd[:, :, toks(2 * p, 2)]).then_inc(ld_x[p], 16)
                if p == 0:
                    sp.dma_start(wqkv_s[:, :, :], wqkv.rearrange("(k p) n -> p k n", p=P)).then_inc(ld_wqkv, 16)
            sp.dma_start(const[:, :], consts).then_inc(ld_const, 16)
            sp.dma_start(tw2_s[:, :, :], tw2.rearrange("(k p) n -> p k n", p=P)).then_inc(ld_tw2, 16)
            for n in range(CHUNKS):
                if n >= W_RING:
                    sp.wait_ge(wl_ready, n - W_RING + 1)
                sp.dma_start(w_s[:, n % W_RING, :], weights[:, n, :]).then_inc(ld_w[n % W_RING], 16)
            od = out_t.rearrange("(k p) n -> p k n", p=P)
            for n, (m, cols) in enumerate(y_parts):
                sp.wait_ge(y_ready, n + 1)
                sp.dma_start(od[:, m, cols], x[:, m, cols]).then_inc(stored, 16)
            sp.wait_ge(stored, 16 * len(y_parts))

        @block.tensor
        def _(pe):
            def a_slot(key):
                n = A_AT[key]
                if n >= 2:
                    pe.wait_ge(a_free, n - 1)
                return a_ring[n % 2]

            def v_slot(key):
                n = V_AT[key]
                if n >= 2:
                    pe.wait_ge(v_free, n - 1)
                return v_ring[n % 2]

            def three_pass(dst, pairs, first=True, last=True):
                terms = [t for wh, wl, xh, xl in pairs for t in ((wh, xh), (wh, xl), (wl, xh))]
                for n, (w, d) in enumerate(terms):
                    mm = pe.matmul(dst, w, d, start=first and n == 0, stop=last and n == len(terms) - 1)
                return mm

            def scales(tw, ld, dst, done):
                pe.wait_ge(ld, 16)
                for m in range(KT):
                    for k in range(KT):
                        mm = pe.matmul(dst[:, m * B:(m + 1) * B], tw[:, k, m * P:(m + 1) * P],
                                       small[:, C_COND + k * B:C_COND + (k + 1) * B], start=k == 0, stop=k == KT - 1)
                mm.then_inc(done, 1)

            def project(b):
                pe.wait_ge(xh_ready, b // 2 + 1)
                if b < 2:
                    pe.wait_ge(xl_ready, 1)
                else:
                    pe.wait_ge(xl_late_ready, b // 2)
                if b >= 3:
                    pe.wait_ge(qkv_read, 1 if b == 3 else b)
                dst = qkv_of(b)[:, 0:QKV]
                terms = [t for k in range(KT) for t in (
                    (norm_h[:, k, toks(b)], wqkv_h[:, k, :]), (norm_l[:, k, toks(b)], wqkv_h[:, k, :]),
                    (norm_h[:, k, toks(b)], wqkv_l[:, k, :]))]
                for n, (w, d) in enumerate(terms):
                    mm = pe.matmul(dst, w, d, start=n == 0, stop=n == len(terms) - 1)
                mm.then_inc(qkv_done, 1)

            def turn_key(b):
                pe.wait_ge(hi_ready, 2 * (b + 1))
                if b in DVE_LO:
                    pe.wait_ge(dve_lo_ready, 2 * (DVE_LO.index(b) + 1))
                else:
                    pe.wait_ge(lo_ready, los_of(b))
                dst = a_slot(("k", b))
                pe.transpose(dst[0:KD, 0:S], parts[:, b % 2, HEADS, :, :].rearrange("p a d -> p (a d)").bitcast(F32),
                             ident).then_inc(a_full, 1)

            def turn_queries(b, g):
                dst = a_slot(("q", b, g))
                for j in range(4):
                    mm = pe.transpose(dst[0:KD, j * S:(j + 1) * S],
                                      parts[:, b % 2, 4 * g + j, :, :].rearrange("p a d -> p (a d)").bitcast(F32), ident)
                mm.then_inc(a_full, 1)

            def scores(b, g):
                pe.wait_ge(a_free, A_AT[("q", b, g)] + 1)
                dst = v_slot(("s1", b, g))
                for j in range(4):
                    mm = pe.matmul(dst[:, j * S:(j + 1) * S], q_t[0:KD, b % QK_RING, 4 * g + j, :], k_t[0:KD, b % QK_RING, :],
                                   start=True, stop=True)
                mm.then_inc(v_full, 1)

            def turn_top(p):
                pe.wait_ge(top_ready, p + 1)
                dst = a_slot(("top", p))
                pe.matmul(dst[KD:P, 0:S], top_parts[:, p % 2, :, :, :].rearrange("p a b h -> p (a b h)").bitcast(F32),
                          ident, start=True, stop=True, tile_position=(0, KD)).then_inc(a_full, 1)

            def scores_t(b, g):
                pe.wait_ge(rows_ready, 2 * b + g + 1)
                n = 2 * b + g
                if n >= 2:
                    pe.wait_ge(s_free, n - 1)
                elif n == 0:
                    pe.wait_ge(qkv_read, 3)
                dst = s_ring[n % 2][:, :]
                heads = slice(4 * g, 4 * g + 4)
                pe.matmul(dst, k_t[:, b % QK_RING, :], q_t[:, b % QK_RING, heads, :].rearrange("p h t -> p (h t)"),
                          start=True, stop=True).then_inc(s_full, 1)

            def values(b):
                pe.wait_ge(s_free, 2 * b + 2)
                if b == B - 3:
                    pe.wait_ge(qkv_read, B)
                elif b >= 1:
                    pe.wait_ge(ctxn_ready, b if b < B - 3 else b - 1)
                for n, w in enumerate((v[:, b, :], ones[:, 0:HD])):
                    for t in range(KT):
                        for j in range(4):
                            at = n * KT * S + t * S
                            mm = pe.matmul(pv_of(b)[HD * j:HD * (j + 1), at:at + S], w, prob[:, b % 2, 4 * t + j, :],
                                           start=True, stop=True, tile_position=(0, HD * j))
                mm.then_inc(pv_done, 1)

            def out_project(h, m):
                pe.wait_ge(wl_ready, 1)
                pe.wait_ge(ctxh_ready, HB * (h + 1))
                pe.wait_ge(ctxl_ready, HB * (h + 1) - h)
                if h:
                    pe.wait_ge(ctxl_last_ready, 1)
                dst = pv_of(B - 2 + m) if h else v_slot(("wo", h, m))
                cols = [slice(k * D + m * P, k * D + (m + 1) * P) for k in range(KT)]
                three_pass(dst[:, :], [(w_h[:, 0, cols[k]], w_l[:, 0, cols[k]], ctx_h[:, k, half(h)], ctx_l[:, k, half(h)])
                                       for k in range(KT)]).then_inc(wo1_done if h else v_full, 1)

            def sum_squares():
                dst = a_slot(("ss", 0))
                for k in range(KT):
                    pe.wait_ge(sq2_ready, k + 1)
                    mm = pe.matmul(dst[:, :], ones[:, :], square[:, k, :], start=k == 0, stop=k == KT - 1)
                mm.then_inc(a_full, 1)

            def sum_squares_cut():
                pe.wait_ge(onesr_ready, 1)
                pe.wait_ge(sq2h_ready, 1)
                pe.wait_ge(sq2l_ready, 1)
                dst = a_slot(("ss", 1))
                pe.matmul(dst[:, :], ones_r[:, :], square_h[:, :], start=True, stop=False)
                pe.matmul(dst[:, :], ones_r[:, :], square_l[:, :], start=False, stop=True).then_inc(a_full, 1)

            def gate_up(h, i):
                pe.wait_ge(wl_ready, gate_chunk(i) + 2)
                for slot, key, n, full in ((a_slot, "g", gate_chunk(i), a_full), (v_slot, "u", gate_chunk(i) + 1, v_full)):
                    dst = slot((key, h, i))
                    cols = [slice(k * 2 * P + i % 2 * P, k * 2 * P + i % 2 * P + P) for k in range(KT)]
                    for k in range(KT):
                        if i == 0 and key == "g":
                            pe.wait_ge(h2h_ready, KT * h + k + 1)
                            pe.wait_ge(h2l_ready, KT * h + k + 1)
                        mm = three_pass(dst[:, :], [(w_h[:, n, cols[k]], w_l[:, n, cols[k]], norm_h[:, k, half(h)], norm_l[:, k, half(h)])],
                                        first=k == 0, last=k == KT - 1)
                    mm.then_inc(full, 1)

            def down(h, i):
                n = h * IT + i
                chunk = gate_chunk(i) + 2
                pe.wait_ge(wl_ready, chunk + 1)
                pe.wait_ge(actl_ready, n + 1)
                if i == 0 and h == 0:
                    pe.wait_ge(s_free, 2 * B)
                if i == 0 and h == 1:
                    pe.wait_ge(y_ready, KT)
                for m in range(KT):
                    r = slice(i % 2 * D + m * P, i % 2 * D + (m + 1) * P)
                    mm = three_pass(s_ring[m][:, :], [(w_h[:, chunk, r], w_l[:, chunk, r], act_h[:, n % 3, :], act_l[:, n % 3, :])],
                                    first=i == 0, last=i == IT - 1)
                    if m == 0 and i == IT - 1:
                        mm.then_inc(down0_done, 1)
                mm.then_inc(down_done, 1)

            def warm_up(n):
                for _ in range(n):
                    pe.matmul(s_ring[0][:, 0:P], ones[:, :], ones[:, :], start=True, stop=True)

            def first_squares(p):
                pe.wait_ge(sq_ready, p + 1)
                for b in range(2):
                    for k in range(KT):
                        mm = pe.matmul(pv_bank[:, 2 * p + b:2 * p + b + 1], square[:, k, toks(2 * (p % 2) + b)], ones[:, 0:1],
                                       start=k == 0, stop=k == KT - 1)
                mm.then_inc(ss_done, 1)

            pe.wait_ge(ones_ready, 1)
            warm_up(WARM_UPS[0])
            pe.wait_ge(ld_small, 16)
            scales(tw1_s, ld_tw1, v_ring[0], scale1_done)
            warm_up(WARM_UPS[1])
            pe.wait_ge(wqkvh_ready, 1)
            pe.wait_ge(wqkvl_ready, 1)
            project(0)
            first_squares(0)
            project(1)
            scales(tw2_s, ld_tw2, v_ring[1], scale2_done)
            first_squares(1)
            warm_up(WARM_UPS[2])
            pe.wait_ge(ld_const, 16)
            for s in range(B):
                turn_key(s)
                turn_queries(s, 0)
                if s == 3:
                    pe.wait_ge(sel_ready, QK_RING // 2)
                if s >= 3:
                    scores_t(s - 3, 0)
                turn_queries(s, 1)
                if s >= 3:
                    scores_t(s - 3, 1)
                if s % 2 == 0 and s >= 2:
                    turn_top(s // 2 - 1)
                if s == 0:
                    project(2)
                    first_squares(2)
                    pe.wait_ge(gain1_ready, KT)
                    pe.wait_ge(gain2_ready, KT)
                if s == 2:
                    first_squares(3)
                scores(s, 0)
                if s >= 3:
                    scores(s, 1)
                if 1 <= s < B - 2:
                    project(s + 2)
                if s == 3:
                    pe.wait_ge(ln1_ready, PAIRS)
                if s >= 3:
                    values(s - 3)
                else:
                    scores(s, 1)
            turn_top(PAIRS - 1)
            out_project(0, 0)
            scores_t(B - 3, 0)
            out_project(0, 1)
            scores_t(B - 3, 1)
            scores_t(B - 2, 0)
            sum_squares()
            scores_t(B - 2, 1)
            values(B - 3)
            values(B - 2)
            scores_t(B - 1, 0)
            scores_t(B - 1, 1)
            gate_up(0, 0)
            values(B - 1)
            gate_up(0, 1)
            out_project(1, 0)
            out_project(1, 1)
            for h in range(2):
                for i in range(IT):
                    if h == 1 or i >= 2:
                        gate_up(h, i)
                    if i >= 2:
                        down(h, i - 2)
                    if h == 0 and i == 4:
                        sum_squares_cut()
                down(h, IT - 2)
                down(h, IT - 1)

        @block.scalar
        def _(act_e):
            act_e.dma_start(pos_i[:, :], pos).then_inc(ld_pos, 16)

            def copy(dst, src):
                return nc.scalar.activation(dst, src, ACT.Copy)

            def cut_x(p):
                if p < 2:
                    act_e.wait_ge(xg_ready, p + 1)
                else:
                    act_e.wait_ge(xg_late_ready, p - 1)
                copy(norm_h[:, :, toks(2 * p, 2)], norm[:, :, toks(2 * (p % 2), 2)]).then_inc(xh_ready, 1)

            def square_x(p):
                act_e.wait_ge(ld_x[p], 16)
                if p >= 2:
                    act_e.wait_ge(ss_done, p - 1)
                nc.scalar.activation(square[:, :, toks(2 * (p % 2), 2)], x[:, :, toks(2 * p, 2)], ACT.Square).then_inc(sq_ready, 1)

            def cut_weight(n):
                act_e.wait_ge(ld_w[n % W_RING], 16 * (n // W_RING + 1))
                copy(w_h[:, n, :], w_s[:, n % W_RING, :]).then_inc(wh_ready, 1)

            def take(key):
                n = A_AT[key]
                act_e.wait_ge(a_full, n + 1)
                return a_ring[n % 2]

            def take_key(b):
                if b >= QK_RING:
                    act_e.wait_ge(s_full, 2 * (b - QK_RING) + 2)
                src = take(("k", b))
                copy(k_t[0:KD, b % QK_RING, :], src[0:KD, 0:S]).then_inc(a_free, 1)

            def take_queries(b, g):
                src = take(("q", b, g))
                copy(q_t[0:KD, b % QK_RING, 4 * g:4 * g + 4, :],
                     src[0:KD, :].rearrange("p (h t) -> p h t", h=4)).then_inc(a_free, 1)

            def take_top(p):
                src = take(("top", p))
                if p >= 2:
                    act_e.wait_ge(rows_ready, 4 * (p - 1))
                copy(top_t[KD:P, p % 2, :], src[KD:P, 0:S]).then_inc(a_free, 1)

            def exps(b, g):
                if b >= 2 and g == 0:
                    act_e.wait_ge(pv_done, b - 1)
                n = 2 * b + g
                act_e.wait_ge(s_full, n + 1)
                nc.scalar.activation(prob[:, b % 2, 4 * g:4 * g + 4, :], s_ring[n % 2][:, :].rearrange("p (h t) -> p h t", h=4),
                                     ACT.Exp, scale=SCALE).then_inc(s_free, 1)

            def log_sums(b):
                act_e.wait_ge(pv_done, b + 1)
                if b >= 1:
                    act_e.wait_ge(suminv_ready, b)
                nc.scalar.activation(sum_ln[:, :], pv_of(b)[:, KT * S:2 * KT * S], ACT.Ln).then_inc(sumln_ready, 1)

            def invert_sums(b):
                act_e.wait_ge(sumln_ready, b + 1)
                if b >= 2:
                    act_e.wait_ge(ctxn_ready, b - 1)
                nc.scalar.activation(sum_inv[:, b % 2, :], sum_ln[:, :], ACT.Exp, scale=-1.0).then_inc(suminv_ready, 1)

            def cut_ctx(b):
                act_e.wait_ge(ctxn_ready, b + 1)
                copy(ctx_h[:, :, toks(b)], ctx_n[:, b % 2, :, :]).then_inc(ctxh_ready, 1)

            def square_x2(h, m):
                if h:
                    act_e.wait_ge(a_full, A_AT[("ss", 0)] + 1)
                    act_e.wait_ge(x2_ready, m + 1)
                else:
                    act_e.wait_ge(ss_done, PAIRS)
                    act_e.wait_ge(v_free, V_AT[("wo", 0, m)] + 1)
                nc.scalar.activation(square[:, m, :], x[:, m, half(h)], ACT.Square).then_inc(sq2_ready, 1)

            def root2(h):
                src = take(("ss", h))
                if h:
                    act_e.wait_ge(h2_ready, KT * h)
                nc.scalar.activation(rstd2[:, :], src[:, :], ACT.Ln, scale=1.0 / D, bias=eps[:, 0:1]).then_inc(a_free, 1)
                act_e.wait_ge(a_free, A_AT[("ss", h)] + 1)
                nc.scalar.activation(rstd2[:, :], rstd2[:, :], ACT.Exp, scale=-0.5).then_inc(rstd2_ready, 1)

            def cut_h2(h):
                for k in range(KT):
                    act_e.wait_ge(h2_ready, KT * h + k + 1)
                    copy(norm_h[:, k, half(h)], norm[:, k, :]).then_inc(h2h_ready, 1)

            def silu(h, i):
                n = h * IT + i
                src = take(("g", h, i))
                if n >= 2:
                    act_e.wait_ge(v_free, V_AT[("u",) + divmod(n - 2, IT)] + 1)
                nc.scalar.activation(gate[:, n % 2, :], src[:, :], ACT.Silu).then_inc(a_free, 1)

            def root1(p):
                act_e.wait_ge(ss_done, p + 1)
                r = slice(2 * p, 2 * p + 2)
                nc.scalar.activation(rms_ln[:, r], pv_bank[:, r], ACT.Ln, scale=1.0 / D, bias=eps[:, 0:1]).then_inc(ln1_ready, 1)
                act_e.wait_ge(ln1_ready, p + 1)
                nc.scalar.activation(rstd1[:, r], rms_ln[:, r], ACT.Exp, scale=-0.5).then_inc(rstd1_ready, 1)

            def cut_weights(n):
                for i in range(n):
                    if chunk[0] < CHUNKS:
                        cut_weight(chunk[0])
                        chunk[0] += 1

            act_e.wait_ge(eps_ready, 1)
            nc.scalar.preload_act_table_set(SIN_TABLE)
            square_x(0)
            act_e.wait_ge(ld_wqkv, 16)
            copy(wqkv_h[:, :, :], wqkv_s[:, :, :]).then_inc(wqkvh_ready, 1)
            cut_x(0)
            act_e.wait_ge(tab_step, TAB_STEPS)
            nc.scalar.activation(trig[:, 0:2, :, :], wrap[:, :, :, :], ACT.Sin).then_inc(trig_ready, 1)
            nc.scalar.activation(trig[:, 2, :, :], wrap[:, 0, :, :], ACT.Sin, scale=-1.0).then_inc(trig_ready, 1)
            nc.scalar.preload_act_table_set("natural_log_exp_and_others")
            root1(0)
            square_x(1)
            cut_x(1)
            square_x(2)
            root1(1)
            chunk = [0]
            for s in range(B):
                if s >= 4:
                    log_sums(s - 4)
                take_key(s)
                if s >= 4:
                    invert_sums(s - 4)
                take_queries(s, 0)
                take_queries(s, 1)
                if s % 2 == 0 and s >= 2:
                    take_top(s // 2 - 1)
                if s >= 3:
                    exps(s - 3, 0)
                    exps(s - 3, 1)
                if s >= 4:
                    cut_ctx(s - 4)
                if s == 0:
                    root1(2)
                    cut_x(2)
                if s == 1:
                    square_x(3)
                    cut_x(3)
                if s == 2:
                    root1(3)
                    act_e.wait_ge(ld_const, 16)
                    for r in range(0, QK_RING, 2):
                        copy(k_t[KD:P, r:r + 2, :], const[KD:P, C_SEL:C_SEL + 2 * P].rearrange("p (b n) -> p b n", b=2)).then_inc(sel_ready, 1)
                cut_weights(ACT_WEIGHTS[s])
            log_sums(B - 4)
            invert_sums(B - 4)
            take_top(PAIRS - 1)
            exps(B - 3, 0)
            square_x2(0, 0)
            exps(B - 3, 1)
            square_x2(0, 1)
            exps(B - 2, 0)
            cut_ctx(B - 4)
            root2(0)
            exps(B - 2, 1)
            cut_h2(0)
            log_sums(B - 3)
            invert_sums(B - 3)
            exps(B - 1, 0)
            exps(B - 1, 1)
            cut_ctx(B - 3)
            log_sums(B - 2)
            invert_sums(B - 2)
            cut_ctx(B - 2)
            log_sums(B - 1)
            invert_sums(B - 1)
            cut_ctx(B - 1)
            for h in range(2):
                for i in range(IT):
                    silu(h, i)
                    if h == 0 and i < 3:
                        cut_weights(2)
                    if h == 0 and i == 2:
                        square_x2(1, 0)
                        square_x2(1, 1)
                        act_e.wait_ge(ones_ready, 1)
                        copy(ones_r[:, :], ones[:, :]).then_inc(onesr_ready, 1)
                        act_e.wait_ge(sq2sum_ready, 1)
                        copy(square_h[:, :], square[:, 0, :]).then_inc(sq2h_ready, 1)
                    if h == 0 and i == 4:
                        root2(1)
                        cut_h2(1)

        @block.vector
        def _(dve):
            ve = nc.vector
            table = [0]

            def tab(ins):
                table[0] += 1
                ins.then_inc(tab_step, 1)
                dve.wait_ge(tab_step, table[0])

            def count_turns(count_scale):
                tab(ve.tensor_scalar(turns[:, :, :], angle[:, :, :], count_scale, ROUND, ALU.mult, ALU.add))
                tab(ve.tensor_scalar(turns[:, :, :], turns[:, :, :], -ROUND, None, ALU.add))

            def take_turns(unit):
                for part in (PI_1, PI_2, PI_3):
                    tab(ve.scalar_tensor_tensor(out=angle[:, :, :], in0=turns[:, :, :], scalar=-part * unit,
                                                in1=angle[:, :, :], op0=ALU.mult, op1=ALU.add))

            def gain(scale, c_ln, dst, done, ready):
                dve.wait_ge(done, 1)
                for k in range(KT):
                    ve.tensor_scalar(dst[:, k, :], scale[:, k * B:(k + 1) * B], 1.0, small[:, c_ln + k:c_ln + k + 1],
                                     ALU.add, ALU.mult).then_inc(ready, 1)

            def gain_x(p):
                r = toks(2 * p, 2)
                dve.wait_ge(ld_x[p], 16)
                dve.wait_ge(gain1_ready, KT)
                ve.tensor_tensor(norm[:, :, toks(2 * (p % 2), 2)].rearrange("p k (b t) -> p k b t", b=2),
                                 x[:, :, r].rearrange("p k (b t) -> p k b t", b=2),
                                 gain1[:, :, 2 * p:2 * p + 2].unsqueeze(3).to_broadcast([P, KT, 2, S]),
                                 ALU.mult).then_inc(xg_ready, 1)

            def rest_x(p):
                r = toks(2 * p, 2)
                dve.wait_ge(xh_ready, p + 1)
                ve.tensor_tensor(norm_l[:, :, r], norm[:, :, toks(2 * (p % 2), 2)], norm_h[:, :, r].bitcast(F32), ALU.subtract).then_inc(xl_ready, 1)

            def rotate(b):
                s = b % 2
                dve.wait_ge(qkv_done, b + 1)
                if b >= 2:
                    if b - 2 not in DVE_LO:
                        dve.wait_ge(lo_ready, los_of(b - 2))
                    dve.wait_ge(a_full, A_AT[("q", b - 2, 1)] + 1)
                bank_b = qkv_of(b)
                src = bank_b[:, 0:NR * HD].rearrange("p (h a d) -> p h a d", h=NR, a=2)
                if b == 0:
                    dve.wait_ge(trig_ready, 2)
                ve.tensor_tensor(by_cos[:, :, :].rearrange("p h (a d) -> p h a d", a=2), src,
                                 trig[:, 1, b, :].unsqueeze(1).unsqueeze(1).to_broadcast([P, NR, 2, HALF]),
                                 ALU.mult).then_inc(rope_step, 1)
                dve.wait_ge(rstd1_ready, b // 2 + 1)
                for a, sine in ((0, 2), (1, 0)):
                    ve.scalar_tensor_tensor(out=by_sin[:, :, :].rearrange("p h (a d) -> p h a d", a=2)[:, :, a, :], in0=src[:, :, 1 - a, :],
                                            scalar=rstd1[:, b:b + 1], in1=trig[:, sine, b, :].unsqueeze(1).to_broadcast([P, NR, HALF]),
                                            op0=ALU.mult, op1=ALU.mult).then_inc(rope_step, 1)
                ve.tensor_scalar(v[:, b, :], bank_b[:, NR * HD:QKV], rstd1[:, b:b + 1], None, ALU.mult).then_inc(qkv_read, 1)
                dve.wait_ge(rope_step, 3 * (b + 1))
                ve.scalar_tensor_tensor(out=turned[:, s, :, :], in0=by_cos[:, :, :], scalar=rstd1[:, b:b + 1], in1=by_sin[:, :, :],
                                        op0=ALU.mult, op1=ALU.add).then_inc(turned_ready, 1)
                dve.wait_ge(turned_ready, b + 1)
                ve.tensor_copy(parts[:, s, HEADS, 0:2, :],
                               turned[:, s, HEADS, :].unsqueeze(1).to_broadcast([P, 2, HD])).then_inc(hi_ready, 1)
                ve.tensor_copy(parts[:, s, 0:HEADS, 0:STACK:2, :],
                               turned[:, s, 0:HEADS, :].unsqueeze(2).to_broadcast([P, HEADS, 2, HD])).then_inc(hi_ready, 1)

            def rest_turned(b):
                for n, (heads, lo) in enumerate(((slice(HEADS, NR), 2), (slice(0, HEADS), 1))):
                    dve.wait_ge(hi_ready, 2 * b + n + 1)
                    ve.tensor_tensor(parts[:, b % 2, heads, lo, :], turned[:, b % 2, heads, :],
                                     parts[:, b % 2, heads, 0, :].bitcast(F32), ALU.subtract).then_inc(dve_lo_ready, 1)

            def maxima(b, g):
                n = V_AT[("s1", b, g)]
                dve.wait_ge(v_full, n + 1)
                if g == 0 and b >= 4:
                    dve.wait_ge(top_ready, b // 2 - 1)
                ve.tensor_reduce(top[:, b // 2 % 2, b % 2, 4 * g:4 * g + 4],
                                 v_ring[n % 2][:, :].rearrange("p (h k) -> p h k", h=4), AX.X, ALU.max).then_inc(v_free, 1)

            def cut_top(p):
                dve.wait_ge(v_free, V_AT[("s1", 2 * p + 1, 1)] + 1)
                if p >= 2:
                    dve.wait_ge(a_full, A_AT[("top", p - 2)] + 1)
                ve.tensor_copy(top_parts[:, p % 2, 0, :, :], top[:, p % 2, :, :]).then_inc(top_hi, 1)
                dve.wait_ge(top_hi, p + 1)
                ve.tensor_tensor(top_parts[:, p % 2, 1, :, :], top[:, p % 2, :, :],
                                 top_parts[:, p % 2, 0, :, :].bitcast(F32), ALU.subtract).then_inc(top_ready, 1)

            def norm_ctx(b):
                dve.wait_ge(suminv_ready, b + 1)
                if b >= 2:
                    dve.wait_ge(ctxh_ready, b - 1)
                    dve.wait_ge(ctxl_ready, b - 1)
                ve.tensor_tensor(ctx_n[:, b % 2, :, :].rearrange("p k t -> p (k t)"), pv_of(b)[:, 0:KT * S],
                                 sum_inv[:, b % 2, :], ALU.mult).then_inc(ctxn_ready, 1)

            def residual1(h, m):
                if h:
                    dve.wait_ge(wo1_done, m + 1)
                    src, done = pv_of(B - 2 + m), x2_ready
                else:
                    n = V_AT[("wo", 0, m)]
                    dve.wait_ge(v_full, n + 1)
                    src, done = v_ring[n % 2], v_free
                ve.tensor_tensor(x[:, m, half(h)], src[:, :], x[:, m, half(h)], ALU.add).then_inc(done, 1)

            def scale_h2(h):
                dve.wait_ge(rstd2_ready, h + 1)
                for k in range(KT):
                    dve.wait_ge(xg2_ready, KT * h + k + 1)
                    ve.tensor_tensor(norm[:, k, :], norm[:, k, :], rstd2[:, :], ALU.mult).then_inc(h2_ready, 1)

            def rest_h2(h):
                for k in range(KT):
                    dve.wait_ge(h2h_ready, KT * h + k + 1)
                    ve.tensor_tensor(norm_l[:, k, half(h)], norm[:, k, :], norm_h[:, k, half(h)].bitcast(F32),
                                     ALU.subtract).then_inc(h2l_ready, 1)

            def activate(h, i):
                n = h * IT + i
                at = V_AT[("u", h, i)]
                dve.wait_ge(v_full, at + 1)
                dve.wait_ge(a_free, A_AT[("g", h, i)] + 1)
                if n >= 3:
                    dve.wait_ge(down_done, n - 2)
                ve.tensor_tensor(act[:, n % 2, :], v_ring[at % 2][:, :], gate[:, n % 2, :], ALU.mult).then_inc(v_free, 1)
                dve.wait_ge(v_free, at + 1)
                ve.tensor_copy(act_h[:, n % 3, :], act[:, n % 2, :]).then_inc(acth_ready, 1)
                dve.wait_ge(acth_ready, n + 1)
                ve.tensor_tensor(act_l[:, n % 3, :], act[:, n % 2, :], act_h[:, n % 3, :].bitcast(F32),
                                 ALU.subtract).then_inc(actl_ready, 1)

            def residual2(h):
                for m, cols in y_parts[:KT] if h == 0 else y_parts[KT:]:
                    if m == 0:
                        dve.wait_ge(down0_done, h + 1)
                    else:
                        dve.wait_ge(down_done, IT * (h + 1))
                    ve.tensor_tensor(x[:, m, cols], s_ring[m][:, cols.start - h * HT:cols.stop - h * HT], x[:, m, cols],
                                     ALU.add).then_inc(y_ready, 1)

            ve.memset(eps[:, :], EPS).then_inc(eps_ready, 1)
            dve.wait_ge(ld_pos, 16)
            dve.wait_ge(ld_small, 16)
            tab(ve.tensor_tensor(angle[:, :, :], pos_i[:, :].unsqueeze(2).to_broadcast([P, B, HALF]),
                                 small[:, C_FREQ:C_FREQ + HALF].unsqueeze(1).to_broadcast([P, B, HALF]), ALU.mult))
            count_turns(1.0 / (TWO_PI * COARSE))
            take_turns(COARSE)
            count_turns(1.0 / TWO_PI)
            take_turns(1.0)
            gain(v_ring[0], C_LN1, gain1, scale1_done, gain1_ready)
            gain_x(0)
            ve.tensor_scalar(turns[:, :, :], angle[:, :, :], float(np.pi / 2), -TWO_PI, ALU.is_gt, ALU.mult).then_inc(table_ready, 1)
            tab(ve.tensor_scalar(wrap[:, 0, :, :], angle[:, :, :], PI_LOW, -PI_LOW, ALU.min, ALU.max))
            dve.wait_ge(table_ready, 1)
            ve.scalar_tensor_tensor(out=angle[:, :, :], in0=angle[:, :, :], scalar=float(np.pi / 2), in1=turns[:, :, :],
                                    op0=ALU.add, op1=ALU.add).then_inc(table_ready, 1)
            dve.wait_ge(table_ready, 2)
            tab(ve.tensor_scalar(wrap[:, 1, :, :], angle[:, :, :], PI_LOW, -PI_LOW, ALU.min, ALU.max))
            assert table[0] == TAB_STEPS
            rest_x(0)
            gain_x(1)
            rotate(0)
            rest_turned(0)
            gain(v_ring[1], C_LN2, gain2, scale2_done, gain2_ready)
            for s in range(B):
                if s + 1 < B and s != 1:
                    rotate(s + 1)
                    if s + 1 in DVE_LO:
                        rest_turned(s + 1)
                if s >= 4:
                    norm_ctx(s - 4)
                if s == 0:
                    rotate(2)
                maxima(s, 0)
                maxima(s, 1)
                if s % 2:
                    cut_top(s // 2)
            norm_ctx(B - 4)
            residual1(0, 0)
            residual1(0, 1)
            scale_h2(0)
            rest_h2(0)
            norm_ctx(B - 3)
            norm_ctx(B - 2)
            norm_ctx(B - 1)
            dve.wait_ge(ctxh_ready, B)
            ve.tensor_tensor(ctx_l[:, :, toks(B - 1)], ctx_n[:, (B - 1) % 2, :, :], ctx_h[:, :, toks(B - 1)].bitcast(F32),
                             ALU.subtract).then_inc(ctxl_last_ready, 1)
            for h in range(2):
                for i in range(IT):
                    activate(h, i)
                    if h == 0 and i == 1:
                        residual1(1, 0)
                        residual1(1, 1)
                    if h == 0 and i == 4:
                        scale_h2(1)
                        rest_h2(1)
                residual2(h)

        @block.gpsimd
        def _(pool):
            gp = nc.gpsimd
            gp.memset(ones[:, :], 1.0).then_inc(ones_ready, 1)

            def rest_weight(n):
                pool.wait_ge(wh_ready, n + 1)
                gp.tensor_tensor(w_l[:, n, :], w_s[:, n % W_RING, :], w_h[:, n, :].bitcast(F32), ALU.subtract).then_inc(wl_ready, 1)

            def gain_x(p):
                r = toks(2 * p, 2)
                pool.wait_ge(ld_x[p], 16)
                pool.wait_ge(gain1_ready, KT)
                pool.wait_ge(xh_ready, p - 1)
                if p == 2:
                    pool.wait_ge(xl_ready, 1)
                else:
                    pool.wait_ge(xl_late_ready, 1)
                gp.tensor_tensor(norm[:, :, toks(2 * (p % 2), 2)].rearrange("p k (b t) -> p k b t", b=2),
                                 x[:, :, r].rearrange("p k (b t) -> p k b t", b=2),
                                 gain1[:, :, 2 * p:2 * p + 2].unsqueeze(3).to_broadcast([P, KT, 2, S]),
                                 ALU.mult).then_inc(xg_late_ready, 1)

            def rest_x(p):
                r = toks(2 * p, 2)
                pool.wait_ge(xh_ready, p + 1)
                gp.tensor_tensor(norm_l[:, :, r], norm[:, :, toks(2 * (p % 2), 2)], norm_h[:, :, r].bitcast(F32), ALU.subtract).then_inc(xl_late_ready, 1)

            def rest_turned(b):
                if b >= 2:
                    pool.wait_ge(a_full, A_AT[("q", b - 2, 1)] + 1)
                for n, (heads, lo) in enumerate(((slice(HEADS, NR), 2), (slice(0, HEADS), 1))):
                    pool.wait_ge(hi_ready, 2 * b + n + 1)
                    gp.tensor_tensor(parts[:, b % 2, heads, lo, :], turned[:, b % 2, heads, :],
                                     parts[:, b % 2, heads, 0, :].bitcast(F32), ALU.subtract).then_inc(lo_ready, 1)

            def spread_top(b, last):
                p = b // 2
                pool.wait_ge(*last)
                pool.wait_ge(a_free, A_AT[("top", p)] + 1)
                if b >= QK_RING:
                    pool.wait_ge(s_full, 2 * (b - QK_RING) + 2)
                for g in range(2):
                    heads = slice(4 * g, 4 * g + 4)
                    gp.tensor_tensor(q_t[KD:P, b % QK_RING, heads, :], top_t[KD:P, p % 2, :].unsqueeze(1).to_broadcast([MROWS, 4, S]),
                                     const[KD:P, C_MASK + 4 * g:C_MASK + 4 * g + 4].unsqueeze(2).to_broadcast([MROWS, 4, S]),
                                     ALU.mult).then_inc(rows_ready, 1)
                pool.wait_ge(rows_ready, 2 * b + 2)

            def rest_ctx(b):
                pool.wait_ge(ctxh_ready, b + 1)
                gp.tensor_tensor(ctx_l[:, :, toks(b)], ctx_n[:, b % 2, :, :], ctx_h[:, :, toks(b)].bitcast(F32),
                                 ALU.subtract).then_inc(ctxl_ready, 1)

            def gain_x2(h):
                if h:
                    pool.wait_ge(h2l_ready, KT)
                for k in range(KT):
                    if h:
                        pool.wait_ge(x2_ready, k + 1)
                    else:
                        pool.wait_ge(v_free, V_AT[("wo", 0, k)] + 1)
                    gp.tensor_tensor(norm[:, k, :].rearrange("p (b t) -> p b t", b=HB), x[:, k, half(h)].rearrange("p (b t) -> p b t", b=HB),
                                     gain2[:, k, HB * h:HB * (h + 1)].unsqueeze(2).to_broadcast([P, HB, S]),
                                     ALU.mult).then_inc(xg2_ready, 1)

            def add_squares2():
                pool.wait_ge(sq2_ready, 2 * KT)
                gp.tensor_tensor(square[:, 0, :], square[:, 0, :], square[:, 1, :], ALU.add).then_inc(sq2sum_ready, 1)

            def rest_squares2():
                pool.wait_ge(sq2h_ready, 1)
                gp.tensor_tensor(square_l[:, :], square[:, 0, :], square_h[:, :].bitcast(F32), ALU.subtract).then_inc(sq2l_ready, 1)

            pool.wait_ge(wqkvh_ready, 1)
            gp.tensor_tensor(wqkv_l[:, :, :], wqkv_s[:, :, :], wqkv_h[:, :, :].bitcast(F32), ALU.subtract).then_inc(wqkvl_ready, 1)
            gain_x(2)
            rest_x(1)
            gain_x(3)
            chunk = 0
            for s in range(B):
                if s == 2:
                    pool.wait_ge(ld_const, 16)
                if s == B - 1:
                    rest_ctx(s - 4)
                    last = (ctxl_ready, s - 3)
                if s + 1 < B and s != 1 and s + 1 not in DVE_LO:
                    rest_turned(s + 1)
                    last = (lo_ready, los_of(s + 1))
                if s >= 2:
                    spread_top(s - 2, last)
                if s == 0:
                    rest_turned(2)
                    last = (lo_ready, los_of(2))
                if s < 2:
                    rest_x(s + 2)
                if 4 <= s < B - 1:
                    rest_ctx(s - 4)
                    last = (ctxl_ready, s - 3)
                for _ in range(POOL_WEIGHTS[s]):
                    rest_weight(chunk)
                    chunk += 1
                    last = (wl_ready, chunk)
            spread_top(B - 2, last)
            pool.wait_ge(gain2_ready, KT)
            gain_x2(0)
            spread_top(B - 1, (xg2_ready, KT))
            for b in range(B - 4, B - 1):
                rest_ctx(b)
            for n in range(chunk, CHUNKS):
                rest_weight(n)
            add_squares2()
            gain_x2(1)
            rest_squares2()


def kernel(x, pos_BxS, cond_2048, L0_cond_ln1_w, L0_cond_ln1_tw, L0_cond_ln2_w, L0_cond_ln2_tw,
           L0_cond_Wq, L0_cond_Wk, L0_cond_Wv, L0_cond_Wo, L0_cond_Wg, L0_cond_Wu, L0_cond_Wd):
    import concourse.bacc as _bacc
    from concourse import mybir as _mybir
    from concourse.bass_utils import run_bass_kernel_spmd as _run

    def rows(a):
        a = np.asarray(a)
        return a.reshape(KT, P, -1).transpose(1, 0, 2).reshape(P, -1)

    def turned(a):
        return np.ascontiguousarray(np.asarray(a).T)

    freq = (np.float32(1.0) / np.float32(ROPE_BASE) ** (np.arange(0, HD, 2, dtype=np.float32) / np.float32(HD))).astype(np.float32)
    const = np.zeros((P, C_CONST), np.float32)
    const[:, C_IDENT:C_IDENT + P] = np.eye(P, dtype=np.float32)
    for r in range(MROWS):
        const[KD + r, C_MASK + r % HEADS] = -1.0
        b = r // HEADS % 2
        const[KD + r, C_SEL + b * P:C_SEL + (b + 1) * P] = 1.0

    w_gate, w_up, w_down = rows(turned(L0_cond_Wg)), rows(turned(L0_cond_Wu)), np.asarray(L0_cond_Wd).T
    chunks = [rows(turned(L0_cond_Wo))]
    for c in range(IT // 2):
        for w in (w_gate, w_up):
            chunks.append(w.reshape(P, KT, INTER)[:, :, 2 * P * c:2 * P * (c + 1)].reshape(P, WIDE))
        chunks.append(w_down[2 * P * c:2 * P * (c + 1)].reshape(2, P, D).transpose(1, 0, 2).reshape(P, WIDE))
    arrays = {
        "smalls": np.concatenate([rows(turned(cond_2048)), rows(np.asarray(L0_cond_ln1_w)[:, None]),
                                  rows(np.asarray(L0_cond_ln2_w)[:, None]), np.broadcast_to(freq, (P, HALF))], axis=1),
        "pos": turned(pos_BxS),
        "x_t": turned(np.asarray(x).reshape(T, D)),
        "tw1": turned(L0_cond_ln1_tw),
        "tw2": turned(L0_cond_ln2_tw),
        "wqkv": np.concatenate([turned(L0_cond_Wq), turned(L0_cond_Wk), turned(L0_cond_Wv)], axis=1),
        "weights": np.stack(chunks, axis=1),
        "consts": const,
    }
    nc = _bacc.Bacc("TRN2", target_bir_lowering=False, num_devices=1)
    feeds, args = {}, []
    for name, a in arrays.items():
        a = np.ascontiguousarray(a)
        feeds[f"in_{name}"] = a
        args.append(nc.dram_tensor(f"in_{name}", a.shape, _mybir.dt.from_np(a.dtype), kind="ExternalInput").ap())
    out = nc.dram_tensor("out_t", (D, T), _mybir.dt.float32, kind="ExternalOutput").ap()
    block_program(nc, *args, out)
    r = _run(nc, [feeds], core_ids=[0])
    return np.ascontiguousarray(np.asarray(r.results[0]["out_t"]).T).reshape(B, S, D)
```
